# Optimizing a Trainium2 kernel written in Bass

```python
import numpy as np
import jax
import jax.numpy as jnp

def _softmax(x, axis=-1):
    return jax.nn.softmax(x, axis=axis)

def _gelu(x):
    return jax.nn.gelu(x, approximate=True)

def _silu(x):
    return jax.nn.silu(x)

def _sigmoid(x):
    return jax.nn.sigmoid(x)

def _layernorm(x, axis=-1, eps=1e-05):
    m = jnp.mean(x, axis=axis, keepdims=True)
    v = jnp.var(x, axis=axis, keepdims=True)
    return (x - m) / jnp.sqrt(v + eps)

def _scatter_add(tgt, idx, src, axis=0):
    return tgt.at[idx].add(src)

def _segment_sum(src, seg, n):
    return jax.ops.segment_sum(src, seg, n)
kernel_name = 'mk_audio_tower_d1_tok_audfeat512_r4_853c15'

def setup_inputs(seed: int=0):
    np.random.seed(seed)
    _w = jnp.asarray

    def _rec_inputs():
        import jax
        import jax.numpy as jnp
        _rk = jax.random.key(seed)
        x = -0.000124254 + 0.999853 * jax.random.normal(jax.random.fold_in(_rk, 1), (8, 64, 1000), jnp.float32)
        return x
    x = _rec_inputs()

    def _L0_tok_setup():
        import jax, jax.numpy as jnp
        import numpy as np
        key = jax.random.key(seed)
        k_x, k_w1, k_w2 = jax.random.split(key, 3)
        P = 200
        in_f = 2 * (P // 2 + 1)
        hid = 4 * in_f
        D = 128
        x = jax.random.normal(k_x, (128, 64, 1000), dtype=jnp.float32)
        W1 = jax.random.normal(k_w1, (in_f, hid), dtype=jnp.float32) * (1.0 / np.sqrt(in_f))
        b1 = jnp.zeros((hid,), dtype=jnp.float32)
        W2 = jax.random.normal(k_w2, (hid, D), dtype=jnp.float32) * (1.0 / np.sqrt(hid))
        b2 = jnp.zeros((D,), dtype=jnp.float32)
        return {'x': x, 'W1': W1, 'b1': b1, 'W2': W2, 'b2': b2, 'patch_size': P}
    _L0_tok_all = _L0_tok_setup()
    _L0_tok_in = {k: v for k, v in _L0_tok_all.items() if k in ('W1', 'b1', 'W2', 'b2')}
    del _L0_tok_all

    def _L0_attn_setup():
        import jax, jax.numpy as jnp
        import numpy as np
        D_MODEL, D_STATE, BATCH, SEQ = (128, 32, 8, 1024)

        def _hippo(n):
            i = np.arange(n)[:, None].astype(np.float64)
            j = np.arange(n)[None, :].astype(np.float64)
            P = np.where(i > j, np.sqrt(2 * i + 1) * np.sqrt(2 * j + 1), 0.0)
            P = P + np.diag(np.arange(1, n + 1).astype(np.float64))
            return (-P).astype(np.float32)

        def _reference_tuple_inner(x, A, B, C, D, log_dt, W_out, b_out):
            n = A.shape[0]
            dt = jnp.mean(jnp.clip(jnp.exp(log_dt), 0.0001, 1.0))
            I = jnp.eye(n, dtype=x.dtype)
            inv_term = jnp.linalg.inv(I - 0.5 * dt * A)
            A_bar = (I + 0.5 * dt * A) @ inv_term
            B_bar = dt * (inv_term @ B)
            uB = jnp.einsum('bsd,nd->bsn', x, B_bar)
            s0 = jnp.zeros((x.shape[0], n), dtype=x.dtype)

            def step(state, ub_t):
                state = jnp.tanh(state @ A_bar.T + ub_t)
                return (state, state)
            final_state, states = jax.lax.scan(step, s0, jnp.swapaxes(uB, 0, 1))
            states = jnp.swapaxes(states, 0, 1)
            y = jnp.einsum('bsn,dn->bsd', states, C) + x * D
            y = y @ W_out.T + b_out
            return (y, final_state)
        key = jax.random.key(seed)
        k0, k1, k2, k3 = jax.random.split(key, 4)
        x = jax.random.normal(k0, (BATCH, SEQ, D_MODEL), dtype=jnp.float32)
        A = jnp.asarray(_hippo(D_STATE))
        B = jax.random.normal(k1, (D_STATE, D_MODEL), dtype=jnp.float32) / np.float32(np.sqrt(D_MODEL))
        C = jax.random.normal(k2, (D_MODEL, D_STATE), dtype=jnp.float32) / np.float32(np.sqrt(D_STATE))
        D = jnp.ones((D_MODEL,), dtype=jnp.float32)
        log_dt = jnp.zeros((D_MODEL,), dtype=jnp.float32)
        W_out = jax.random.normal(k3, (D_MODEL, D_MODEL), dtype=jnp.float32) / np.float32(np.sqrt(D_MODEL))
        b_out = jnp.zeros((D_MODEL,), dtype=jnp.float32)
        return {'x': x, 'A': A, 'B': B, 'C': C, 'D': D, 'log_dt': log_dt, 'W_out': W_out, 'b_out': b_out}
    _L0_attn_all = _L0_attn_setup()
    _L0_attn_in = {k: v for k, v in _L0_attn_all.items() if k in ('A', 'B', 'C', 'D', 'log_dt', 'W_out', 'b_out')}
    del _L0_attn_all

    def _L0_ffn_setup():
        import jax, jax.numpy as jnp
        import numpy as np
        B, T, D, H = (64, 128, 128, 256)

        def _linear_params(key, out_dim, in_dim):
            kw, kb = jax.random.split(key)
            bound = 1.0 / np.sqrt(in_dim)
            W = jax.random.uniform(kw, (out_dim, in_dim), jnp.float32, -bound, bound)
            b = jax.random.uniform(kb, (out_dim,), jnp.float32, -bound, bound)
            return (W, b)
        key = jax.random.key(seed)
        ks = jax.random.split(key, 8)
        x = jax.random.normal(ks[0], (B, T, D), jnp.float32)
        Wuz, buz = _linear_params(ks[1], H, D)
        Wwz, bwz = _linear_params(ks[2], H, H)
        Wur, bur = _linear_params(ks[3], H, D)
        Wwr, bwr = _linear_params(ks[4], H, H)
        Wu, bu = _linear_params(ks[5], H, D)
        Ww, bw = _linear_params(ks[6], H, H)
        Wo, bo = _linear_params(ks[7], D, H)
        return dict(x=x, Wuz=Wuz, buz=buz, Wwz=Wwz, bwz=bwz, Wur=Wur, bur=bur, Wwr=Wwr, bwr=bwr, Wu=Wu, bu=bu, Ww=Ww, bw=bw, Wo=Wo, bo=bo)
    _L0_ffn_all = _L0_ffn_setup()
    _L0_ffn_in = {k: v for k, v in _L0_ffn_all.items() if k in ('Wuz', 'buz', 'Wwz', 'bwz', 'Wur', 'bur', 'Wwr', 'bwr', 'Wu', 'bu', 'Ww', 'bw', 'Wo', 'bo')}
    del _L0_ffn_all
    return {'x': x, 'L0_tok_W1': _L0_tok_in['W1'], 'L0_tok_b1': _L0_tok_in['b1'], 'L0_tok_W2': _L0_tok_in['W2'], 'L0_tok_b2': _L0_tok_in['b2'], 'L0_attn_A': _L0_attn_in['A'], 'L0_attn_B': _L0_attn_in['B'], 'L0_attn_C': _L0_attn_in['C'], 'L0_attn_D': _L0_attn_in['D'], 'L0_attn_log_dt': _L0_attn_in['log_dt'], 'L0_attn_W_out': _L0_attn_in['W_out'], 'L0_attn_b_out': _L0_attn_in['b_out'], 'L0_ffn_Wuz': _L0_ffn_in['Wuz'], 'L0_ffn_buz': _L0_ffn_in['buz'], 'L0_ffn_Wwz': _L0_ffn_in['Wwz'], 'L0_ffn_bwz': _L0_ffn_in['bwz'], 'L0_ffn_Wur': _L0_ffn_in['Wur'], 'L0_ffn_bur': _L0_ffn_in['bur'], 'L0_ffn_Wwr': _L0_ffn_in['Wwr'], 'L0_ffn_bwr': _L0_ffn_in['bwr'], 'L0_ffn_Wu': _L0_ffn_in['Wu'], 'L0_ffn_bu': _L0_ffn_in['bu'], 'L0_ffn_Ww': _L0_ffn_in['Ww'], 'L0_ffn_bw': _L0_ffn_in['bw'], 'L0_ffn_Wo': _L0_ffn_in['Wo'], 'L0_ffn_bo': _L0_ffn_in['bo']}

def reference(x, L0_tok_W1, L0_tok_b1, L0_tok_W2, L0_tok_b2, L0_attn_A, L0_attn_B, L0_attn_C, L0_attn_D, L0_attn_log_dt, L0_attn_W_out, L0_attn_b_out, L0_ffn_Wuz, L0_ffn_buz, L0_ffn_Wwz, L0_ffn_bwz, L0_ffn_Wur, L0_ffn_bur, L0_ffn_Wwr, L0_ffn_bwr, L0_ffn_Wu, L0_ffn_bu, L0_ffn_Ww, L0_ffn_bw, L0_ffn_Wo, L0_ffn_bo):
    import jax
    import jax.numpy as jnp

    def _L0_tok_ref(x, W1, b1, W2, b2, patch_size):
        import jax, jax.numpy as jnp
        import numpy as np
        B, C, T = x.shape
        S = T // patch_size
        xp = x.reshape(B, C, S, patch_size)
        fr = jnp.fft.rfft(xp, axis=-1)
        feats = jnp.concatenate([jnp.abs(fr), jnp.angle(fr)], axis=-1)
        h = jax.nn.gelu(feats @ W1 + b1, approximate=False)
        out = h @ W2 + b2
        return out.reshape(B, C * S, -1)

    def _L0_attn_ref(x, A, B, C, D, log_dt, W_out, b_out):
        import jax, jax.numpy as jnp
        import numpy as np
        D_MODEL, D_STATE, BATCH, SEQ = (128, 32, 8, 1024)

        def _hippo(n):
            i = np.arange(n)[:, None].astype(np.float64)
            j = np.arange(n)[None, :].astype(np.float64)
            P = np.where(i > j, np.sqrt(2 * i + 1) * np.sqrt(2 * j + 1), 0.0)
            P = P + np.diag(np.arange(1, n + 1).astype(np.float64))
            return (-P).astype(np.float32)

        def _reference_tuple_inner(x, A, B, C, D, log_dt, W_out, b_out):
            n = A.shape[0]
            dt = jnp.mean(jnp.clip(jnp.exp(log_dt), 0.0001, 1.0))
            I = jnp.eye(n, dtype=x.dtype)
            inv_term = jnp.linalg.inv(I - 0.5 * dt * A)
            A_bar = (I + 0.5 * dt * A) @ inv_term
            B_bar = dt * (inv_term @ B)
            uB = jnp.einsum('bsd,nd->bsn', x, B_bar)
            s0 = jnp.zeros((x.shape[0], n), dtype=x.dtype)

            def step(state, ub_t):
                state = jnp.tanh(state @ A_bar.T + ub_t)
                return (state, state)
            final_state, states = jax.lax.scan(step, s0, jnp.swapaxes(uB, 0, 1))
            states = jnp.swapaxes(states, 0, 1)
            y = jnp.einsum('bsn,dn->bsd', states, C) + x * D
            y = y @ W_out.T + b_out
            return (y, final_state)
        return _reference_tuple_inner(x, A, B, C, D, log_dt, W_out, b_out)[0]

    def _L0_ffn_ref(x, Wuz, buz, Wwz, bwz, Wur, bur, Wwr, bwr, Wu, bu, Ww, bw, Wo, bo):
        import jax, jax.numpy as jnp
        import numpy as np
        B, T, D, H = (64, 128, 128, 256)

        def _linear_params(key, out_dim, in_dim):
            kw, kb = jax.random.split(key)
            bound = 1.0 / np.sqrt(in_dim)
            W = jax.random.uniform(kw, (out_dim, in_dim), jnp.float32, -bound, bound)
            b = jax.random.uniform(kb, (out_dim,), jnp.float32, -bound, bound)
            return (W, b)
        b_, t_, _ = x.shape
        h_dim = Wwz.shape[0]
        xz = (jnp.einsum('btd,hd->bth', x, Wuz) + buz).transpose(1, 0, 2)
        xr = (jnp.einsum('btd,hd->bth', x, Wur) + bur).transpose(1, 0, 2)
        xc = (jnp.einsum('btd,hd->bth', x, Wu) + bu).transpose(1, 0, 2)

        def step(h, inp):
            xz_t, xr_t, xc_t = inp
            z = jax.nn.sigmoid(xz_t + h @ Wwz.T + bwz)
            r = jax.nn.sigmoid(xr_t + h @ Wwr.T + bwr)
            c = jnp.tanh(xc_t + h * r @ Ww.T + bw)
            h_new = z * h + (1.0 - z) * c
            return (h_new, h_new)
        h0 = jnp.zeros((b_, h_dim), x.dtype)
        _, hs = jax.lax.scan(step, h0, (xz, xr, xc))
        out = jax.nn.sigmoid(jnp.einsum('tbh,dh->btd', hs, Wo) + bo)
        return out
    h = _L0_tok_ref(x, L0_tok_W1, L0_tok_b1, L0_tok_W2, L0_tok_b2, 200)
    h = h + _L0_attn_ref(_layernorm(h, axis=-1), L0_attn_A, L0_attn_B, L0_attn_C, L0_attn_D, L0_attn_log_dt, L0_attn_W_out, L0_attn_b_out)
    h = h + _L0_ffn_ref(_layernorm(h, axis=-1), L0_ffn_Wuz, L0_ffn_buz, L0_ffn_Wwz, L0_ffn_bwz, L0_ffn_Wur, L0_ffn_bur, L0_ffn_Wwr, L0_ffn_bwr, L0_ffn_Wu, L0_ffn_bu, L0_ffn_Ww, L0_ffn_bw, L0_ffn_Wo, L0_ffn_bo)
    return h

_drawn_inputs = setup_inputs


def setup_inputs(seed=0):
    import zlib

    import numpy as np

    out = dict(_drawn_inputs(seed))
    spreads = {'L0_tok_b1': (0.0, 0.726),
     'L0_tok_b2': (0.0, 0.488),
     'L0_attn_D': (1.0, 0.547),
     'L0_attn_log_dt': (0.0, 2.0),
     'L0_attn_b_out': (0.0, 0.527)}
    factors = {'L0_ffn_Wuz': 8.0,
     'L0_ffn_buz': 66.03,
     'L0_ffn_Wwz': 8.0,
     'L0_ffn_bwz': 73.316,
     'L0_ffn_Wur': 8.0,
     'L0_ffn_bur': 63.63,
     'L0_ffn_Wwr': 8.0,
     'L0_ffn_bwr': 78.077,
     'L0_ffn_Wu': 5.63,
     'L0_ffn_bu': 23.399,
     'L0_ffn_Ww': 8.0,
     'L0_ffn_bw': 24.05,
     'L0_ffn_Wo': 5.757,
     'L0_ffn_bo': 61.43}
    for name, (base, spread) in spreads.items():
        noise = np.random.default_rng([zlib.crc32(name.encode()), seed]).standard_normal(out[name].shape)
        drawn = base * np.exp(spread * noise) if base else spread * noise
        out[name] = jnp.asarray(drawn.astype(out[name].dtype))
    for name, factor in factors.items():
        out[name] = (out[name] * factor).astype(out[name].dtype)
    return out
```

```python
from contextlib import ExitStack

import concourse.bass as bass
from concourse import mybir

ALU = mybir.AluOpType
ACT = mybir.ActivationFunctionType
F32 = mybir.dt.float32
BF16 = mybir.dt.bfloat16
F16 = mybir.dt.float16
U32 = mybir.dt.uint32
AX = mybir.AxisListType.X

HALF_PI = 1.5707963267948966
TINY = 1e-30
TINY_POWER = 1e-34
EPS = 1e-5
NEWTON_PER_GROUP = 10


def audio_tower(nc, x, W1, b1, W2, b2, A, Bm, C, D, log_dt, W_out, b_out,
                Wuz, buz, Wwz, bwz, Wur, bur, Wwr, bwr, Wu, bu, Ww, bw, Wo, bo, dft, out):
    NB, NC, LEN = x.shape
    KP = dft.shape[0]
    PATCH = 2 * KP
    NS = LEN // PATCH
    NF = PATCH // 2 + 1
    T = NC * NS
    NT = T * NB
    HID = W1.shape[1]
    DM = W2.shape[1]
    N = A.shape[0]
    H = Wwz.shape[0]
    KH = H // 128
    CH = 16
    CT = CH * NB
    NCH = T // CH
    GT = 512
    NG = NT // GT
    GQ = GT // 128
    MC = -(-HID // 128)
    ML = HID - 128 * (MC - 1)
    PAIR = 2
    NP = NB // PAIR
    PT = NS * PAIR * NC
    HT = PT // 2
    assert CT == 128 and DM == 128 and KH == 2 and PAIR * NC == 128 and HT <= 512 and H == 256

    with ExitStack() as ctx:
        def sb(name, shape, dt=F32):
            return ctx.enter_context(nc.sbuf_tensor(name, shape, dt))

        def sem(name):
            return ctx.enter_context(nc.semaphore(name))

        x_sb = sb("x_sb", [128, NP, LEN])
        dft_sb = sb("dft_sb", [KP, 2, 2, NF])
        ident = sb("ident", [128, 128])
        ident_bf = sb("ident_bf", [128, 128], BF16)
        patT = sb("patT", [KP, 2, PT])
        magT = sb("magT", [NF, NT])
        angT = sb("angT", [NF, NT])
        absre = sb("absre", [NF, PT])
        imag = sb("imag", [NF, NP, PT])
        absim = sb("absim", [NF, NP, PT])
        neghalf = sb("neghalf", [NF, NP, PT])
        re2 = sb("re2", [NF, PT])
        im2 = sb("im2", [NF, PT])
        power = sb("power", [NF, PT])
        denom = sb("denom", [NF, PT])
        rdenom = sb("rdenom", [NF, PT])
        expo_ln = sb("expo_ln", [128, GQ])
        W1_sb = sb("W1_sb", [NF, 2, HID])
        W2_sb = sb("W2_sb", [128, MC, DM])
        bias_rows = sb("bias_rows", [32, 128])
        biasT = sb("biasT", [128, 32])
        gbias = sb("gbias", [128, 3 * KH])
        vec_rows = sb("vec_rows", [1, 3, DM])
        ones_row = sb("ones_row", [1, 128])
        ones_sq = sb("ones_sq", [N, N])
        b2_bc = sb("b2_bc", [128, GQ, DM])
        bout_bc = sb("bout_bc", [128, GQ, DM])
        bo_bc = sb("bo_bc", [128, DM])
        hid = sb("hid", [128, 2, GT])
        h1 = sb("h1", [128, GT])
        h1b = sb("h1b", [128, GT])
        stats = sb("stats", [128, GQ, 6])
        mv = sb("mv", [128, GQ, 2])
        var_eps = sb("var_eps", [128, GQ])
        rstd = sb("rstd", [128, GQ])
        xln = sb("xln", [128, GT])
        xlnT_g = sb("xlnT_g", [128, GT])
        xlnT = sb("xlnT", [128, NT])
        hres = sb("hres", [128, NT])
        Wout_sb = sb("Wout_sb", [128, DM])
        WoutT = sb("WoutT", [128, DM])
        WDT = sb("WDT", [128, DM])
        C_sb = sb("C_sb", [DM, N])
        WCT = sb("WCT", [N, DM])
        Dcol = sb("Dcol", [DM, 1])
        A_sb = sb("A_sb", [N, N])
        AT = sb("AT", [N, N])
        B_sb = sb("B_sb", [N, DM])
        dtrow = sb("dtrow", [1, DM])
        dtsum = sb("dtsum", [1, 1])
        dtcol = sb("dtcol", [128, 1])
        negdt = sb("negdt", [128, 1])
        Mt = sb("Mt", [N, 2, N])
        sq = sb("sq", [N, N])
        sqsum = sb("sqsum", [N, 1])
        scale0 = sb("scale0", [N, 1])
        negMT = sb("negMT", [128, N])
        eye = sb("eye", [128, N])
        eye2 = sb("eye2", [128, N])
        XY = sb("XY", [128, 2, N])
        Dn = sb("Dn", [128, N])
        AbarT = sb("AbarT", [128, N])
        BbarT = sb("BbarT", [DM, N])
        states = sb("states", [128, CT])
        wnat = sb("wnat", [128, 3, KH, H])
        wunat = sb("wunat", [128, 3, KH, DM])
        wonat = sb("wonat", [DM, H])
        wT = sb("wT", [128, 3, KH * H])
        wres = sb("wres", [128, KH * H])
        wparts = sb("wparts", [128, 3, 3, KH, H], BF16)
        WuT = sb("WuT", [128, 3 * KH, 128])
        WoT = sb("WoT", [128, KH, DM])
        h2 = sb("h2", [128, DM])
        stats2 = sb("stats2", [128, 6])
        mv2 = sb("mv2", [128, 2])
        vare2 = sb("vare2", [128, 1])
        rstd2 = sb("rstd2", [128, 1])
        x2 = sb("x2", [128, DM])
        x2T = sb("x2T", [128, CT])
        gin = sb("gin", [128, CH, 3, KH * NB])
        gparts = sb("gparts", [128, 3, CH, 3, KH * NB], BF16)
        gres = sb("gres", [128, 2, CH // 2, KH * NB])
        SW = KH * NB
        tanh_r = sb("tanh_r", [128, SW])
        tanh_z = sb("tanh_z", [128, SW])
        zgate = sb("zgate", [128, SW])
        coef = sb("coef", [128, SW, 2])
        addend = sb("addend", [128, SW, 2])
        h_hi = sb("h_hi", [128, SW, 2], F16)
        h_lo = sb("h_lo", [128, SW], F16)
        hseq = sb("hseq", [128, CH, SW, 2])
        rh = sb("rh", [128, SW])
        rh_hi = sb("rh_hi", [128, SW], F16)
        rh_lo = sb("rh_lo", [128, SW], F16)
        hchunk = sb("hchunk", [128, KH, CH, NB])
        logit = sb("logit", [128, DM])
        tanh_o = sb("tanh_o", [128, DM])
        sig_o = sb("sig_o", [128, DM])
        res = sb("res", [128, DM])

        ps = ctx.enter_context(nc.psum_tensor("ps", [128, 8, 512], F32))

        def bank(i, p=128, w=512):
            return ps[0:p, i, 0:w]

        ps_patT = ps[0:KP, 0:4, :].rearrange("p (k b) w -> p k (b w)", k=2)
        ps_re = ps[0:NF, 4:6, 0:HT]
        ps_im = ps[0:NF, 6:8, 0:HT]
        ps_out, ps_xT, ps_y0 = bank(2), bank(3), bank(4)
        ps_nt, ps_nx = bank(5, N, N), bank(6, N, 2 * N)
        ps_misc = bank(7)
        ps_gate = [bank(g, 128, SW) for g in range(3)]
        ps_s = bank(3, N, CT)
        ps_x = bank(4, 128, 2 * CT)
        ps_p = bank(5, 128, CT)
        ps_o = bank(6, 128, DM)

        x_in = [sem(f"x_in{g}") for g in range(NP)]
        dft_in = sem("dft_in")
        tok_in = sem("tok_in")
        rows_in = sem("rows_in")
        ssm_in = sem("ssm_in")
        gru_in = sem("gru_in")
        consts = sem("consts")
        pool_passed = sem("pool_passed")
        dve_passed = sem("dve_passed")
        bf_ident = sem("bf_ident")
        patT_psum = sem("patT_psum")
        patT_copied = sem("patT_copied")
        spec_psum = sem("spec_psum")
        absre_done = sem("absre_done")
        sp_act = sem("sp_act")
        sp_dve = sem("sp_dve")
        rden_done = sem("rden_done")
        fold_done = sem("fold_done")
        re_read = sem("re_read")
        im_read = sem("im_read")
        tang_done = sem("tang_done")
        atan_done = sem("atan_done")
        sign_done = sem("sign_done")
        ang_done = sem("ang_done")
        su_act = sem("su_act")
        su_dve = sem("su_dve")
        su_pool = sem("su_pool")
        su_pe = sem("su_pe")
        wT_done = sem("wT_done")
        wp_done = sem("wp_done")
        hid_psum = sem("hid_psum")
        gelu_done = sem("gelu_done")
        out_psum = sem("out_psum")
        out_read = sem("out_read")
        st_done = sem("st_done")
        mv_done = sem("mv_done")
        ve_done = sem("ve_done")
        rstd_done = sem("rstd_done")
        xln_done = sem("xln_done")
        xT_psum = sem("xT_psum")
        xT_copied = sem("xT_copied")
        xT_stored = sem("xT_stored")
        h1b_done = sem("h1b_done")
        y0_psum = sem("y0_psum")
        y0_read = sem("y0_read")
        nt_psum = sem("nt_psum")
        dn_done = sem("dn_done")
        nx_psum = sem("nx_psum")
        xy_done = sem("xy_done")
        bar_done = sem("bar_done")
        s_psum = sem("s_psum")
        s_done = sem("s_done")
        p_psum = sem("p_psum")
        h2_done = sem("h2_done")
        st2_done = sem("st2_done")
        mv2_done = sem("mv2_done")
        h2_stored = sem("h2_stored")
        ve2_done = sem("ve2_done")
        rstd2_done = sem("rstd2_done")
        x2_done = sem("x2_done")
        x2T_psum = sem("x2T_psum")
        x2T_done = sem("x2T_done")
        gx_psum = sem("gx_psum")
        gin_done = sem("gin_done")
        gp_chain = sem("gp_chain")
        h_hi_done = sem("h_hi_done")
        h_full = sem("h_full")
        h_lo_done = sem("h_lo_done")
        r_psum = sem("r_psum")
        z_psum = sem("z_psum")
        c_psum = sem("c_psum")
        r_done = sem("r_done")
        z_done = sem("z_done")
        c_done = sem("c_done")
        rh_hi_done = sem("rh_hi_done")
        rh_full = sem("rh_full")
        rh_lo_done = sem("rh_lo_done")
        zg_done = sem("zg_done")
        zh_done = sem("zh_done")
        hchunk_done = sem("hchunk_done")
        o_psum = sem("o_psum")
        logit_done = sem("logit_done")
        tanho_done = sem("tanho_done")
        sigo_done = sem("sigo_done")
        res_done = sem("res_done")
        out_dma = sem("out_dma")

        def group_order(t, g):
            v = t[:, :].rearrange("p (c s b) -> p s b c", c=NC, s=NS, b=NB)
            return v[:, :, PAIR * g:PAIR * g + PAIR, :]

        def tile_order(t):
            return t.rearrange("p (s b c) -> p s b c", s=NS, b=PAIR)

        def msize(m):
            return 128 if m < MC - 1 else ML

        def gate_cols(m):
            return slice(m * NB, (m + 1) * NB)

        def newton_slots():
            q = []
            for i in range(2 * NEWTON_PER_GROUP):
                q.append((i // 2, i % 2))
            while len(q) < 3 * MC:
                q.append(None)
            return q

        SLOTS = newton_slots()
        OUT_T = out.rearrange("b t d -> t b d")
        def atan(act, a, g):
            act.wait_ge(tang_done, g + 1)
            a.activation(absim[:, g, :], absim[:, g, :], ACT.Arctan).then_inc(atan_done, 1)

        def scan(v, dst):
            return v.tensor_tensor_scan(out=dst, data0=coef[:].rearrange("p s i -> p (s i)"),
                                        data1=addend[:].rearrange("p s i -> p (s i)"), initial=0.0,
                                        op0=ALU.mult, op1=ALU.add)

        def denom_add(v, g):
            for s in range(NS):
                last = v.scalar_tensor_tensor(
                    out=tile_order(denom[:])[:, s], in0=tile_order(absre[:])[:, s], scalar=TINY,
                    in1=group_order(magT, g)[:, s], op0=ALU.max, op1=ALU.add)
            last.then_inc(sp_dve, 1)

        def angle(dve, v, g):
            v.tensor_scalar(imag[:, g, :].bitcast(U32), imag[:, g, :].bitcast(U32), 0x80000000, None,
                            ALU.bitwise_and).then_inc(sign_done, 1)
            dve.wait_ge(sign_done, g + 1)
            dve.wait_ge(fold_done, g + 1)
            for s in range(NS):
                last = v.scalar_tensor_tensor(
                    out=group_order(angT, g)[:, s].bitcast(U32),
                    in0=tile_order(neghalf[:, g, :])[:, s].bitcast(U32), scalar=0x7fffffff,
                    in1=tile_order(imag[:, g, :])[:, s].bitcast(U32), op0=ALU.bitwise_and, op1=ALU.bitwise_or)
            last.then_inc(ang_done, 1)

        block = ctx.enter_context(nc.Block())

        @block.sync
        def _(sp):
            sp.dma_start(x_sb[:, 0, :], x[0:PAIR].rearrange("b c n -> (b c) n")).then_inc(x_in[0], 16)
            sp.dma_start(dft_sb[:], dft).then_inc(dft_in, 16)
            for g in range(1, NP):
                sp.dma_start(x_sb[:, g, :],
                             x[PAIR * g:PAIR * g + PAIR].rearrange("b c n -> (b c) n")).then_inc(x_in[g], 16)
            sp.dma_start(W1_sb[:], W1.rearrange("(k p) h -> p k h", p=NF)).then_inc(tok_in, 16)
            sp.dma_start(W2_sb[:, 0:MC - 1, :],
                         W2[0:128 * (MC - 1), :].rearrange("(m p) d -> p m d", p=128)).then_inc(tok_in, 16)
            sp.dma_start(W2_sb[0:ML, MC - 1, :], W2[128 * (MC - 1):HID, :]).then_inc(tok_in, 16)
            for g, (w, u) in enumerate(((Wwr, Wur), (Wwz, Wuz), (Ww, Wu))):
                sp.dma_start(wnat[:, g, :, :], w.rearrange("(m p) k -> p m k", p=128)).then_inc(gru_in, 16)
                sp.dma_start(wunat[:, g, :, :], u.rearrange("(m p) k -> p m k", p=128)).then_inc(gru_in, 16)
            sp.dma_start(wonat[:], Wo).then_inc(gru_in, 16)

            def store(c):
                sp.wait_ge(res_done, c + 1)
                sp.dma_start(OUT_T[bass.ds(c * CH, CH)], res[:]).then_inc(out_dma, 16)

            with sp.Fori(0, NCH) as c:
                store(c)
            sp.wait_ge(out_dma, 16 * NCH)

        @block.gpsimd
        def _(pool):
            pool.memset(ident[:], 0.0).then_inc(su_pool, 1)
            pool.memset(bias_rows[:], 0.0).then_inc(su_pool, 1)
            pool.wait_ge(su_pool, 2)
            pool.affine_select(out=ident[:], in_=ident[:], compare_op=ALU.not_equal, fill=1.0, base=0,
                               pattern=[[-1, 128]], channel_multiplier=1).then_inc(consts, 1)
            pool.dma_start(bias_rows[0:MC - 1, :],
                           b1[0:128 * (MC - 1)].rearrange("(m p) -> m p", p=128)).then_inc(rows_in, 16)
            pool.dma_start(bias_rows[MC - 1:MC, 0:ML],
                           b1[128 * (MC - 1):HID].rearrange("(m p) -> m p", m=1)).then_inc(rows_in, 16)
            for i, v in enumerate((bur, buz, bu, bwr, bwz, bw)):
                r = MC + KH * i
                pool.dma_start(bias_rows[r:r + KH, :],
                               v.rearrange("(m p) -> m p", p=128)).then_inc(rows_in, 16)
            pool.memset(ones_row[:], 1.0).then_inc(consts, 1)
            pool.memset(ones_sq[:], 1.0).then_inc(consts, 1)
            pool.memset(expo_ln[:], -0.5).then_inc(consts, 1)
            for z in (XY[:].rearrange("p a n -> p (a n)"), Dn[:], negMT[:], AbarT[:], states[:]):
                pool.memset(z, 0.0).then_inc(consts, 1)
            pool.memset(coef[:].rearrange("p a n -> p (a n)"), 0.0).then_inc(consts, 1)
            pool.memset(addend[:].rearrange("p a n -> p (a n)"), 0.0).then_inc(consts, 1)
            pool.memset(hseq[:].rearrange("p a b n -> p (a b n)"), 0.0).then_inc(consts, 1)
            pool.memset(h_hi[:].rearrange("p a n -> p (a n)"), 0.0).then_inc(consts, 1)
            pool.memset(h_lo[:], 0.0).then_inc(consts, 1)
            pool.wait_ge(consts, 1)
            pool.tensor_copy(ident_bf[:], ident[:]).then_inc(bf_ident, 1)
            pool.tensor_copy(eye[:], ident[:, 0:N]).then_inc(bf_ident, 1)
            pool.tensor_scalar(eye2[:], ident[:, 0:N], 2.0, None, ALU.mult).then_inc(bf_ident, 1)

            def fold(g):
                pool.wait_ge(atan_done, g + 1)
                pool.tensor_tensor(neghalf[:, g, :], absim[:, g, :], neghalf[:, g, :],
                                   ALU.subtract).then_inc(fold_done, 1)

            for g in range(NP):
                pool.wait_ge(rden_done, g + 1)
                pool.wait_ge(sp_act, 4 * g + 3)
                pool.tensor_tensor(absim[:, g, :], absim[:, g, :], rdenom[:], ALU.mult).then_inc(tang_done, 1)
                if g >= 1:
                    fold(g - 1)
            fold(NP - 1)

            for g in range(3):
                src = wT[:, g, :]
                part = [wparts[:, i, g, :, :].rearrange("p k h -> p (k h)") for i in range(3)]
                pool.wait_ge(wT_done, g + 1)
                pool.tensor_copy(part[0], src).then_inc(wp_done, 1)
                pool.wait_ge(wp_done, 4 * g + 1)
                pool.tensor_tensor(wres[:], src, part[0], ALU.subtract).then_inc(wp_done, 1)
                pool.wait_ge(wp_done, 4 * g + 2)
                pool.tensor_copy(part[1], wres[:]).then_inc(wp_done, 1)
                pool.wait_ge(wp_done, 4 * g + 3)
                pool.tensor_tensor(part[2], wres[:], part[1], ALU.subtract).then_inc(wp_done, 1)
                pool.wait_ge(wp_done, 4 * g + 4)

            def tok_tail(n):
                pool.wait_ge(xT_copied, n + 1)
                pool.sem_inc(pool_passed, 1)
                pool.tensor_copy(xlnT[:, bass.ds(n * GT, GT)], xlnT_g[:]).then_inc(xT_stored, 1)

            def tok_head(n, first):
                if not first:
                    pool.wait_ge(y0_read, n)
                pool.wait_ge(out_read, n + 1)
                pool.tensor_tensor(h1b[:], h1[:], bout_bc[:].rearrange("p q d -> p (q d)"),
                                   ALU.add).then_inc(h1b_done, 1)
                pool.wait_ge(mv_done, n + 1)
                pool.sem_inc(pool_passed, 1)
                pool.tensor_scalar(var_eps[:], mv[:, :, 1], EPS, None, ALU.add).then_inc(ve_done, 1)
                pool.wait_ge(ve_done, n + 1)
                pool.tensor_tensor(rstd[:], var_eps[:], expo_ln[:], ALU.pow).then_inc(rstd_done, 1)

            pool.wait_ge(su_act, 5)
            tok_head(0, True)
            with pool.Fori(1, NG) as n:
                tok_tail(n - 1)
                tok_head(n, False)
            tok_tail(NG - 1)

            def split(c, half, g):
                s0 = half * (CH // 2)
                base = 24 * c + 12 * half + 4 * g
                src = gin[:, s0:s0 + CH // 2, g, :]
                part = [gparts[:, i, s0:s0 + CH // 2, g, :] for i in range(3)]
                pool.wait_ge(gin_done, 6 * c + 2 * g + 2)
                pool.sem_inc(pool_passed, 1)
                pool.tensor_copy(part[0], src).then_inc(gp_chain, 1)
                pool.wait_ge(gp_chain, base + 1)
                pool.tensor_tensor(gres[:, 0], src, part[0], ALU.subtract).then_inc(gp_chain, 1)
                pool.wait_ge(gp_chain, base + 2)
                pool.sem_inc(pool_passed, 1)
                pool.tensor_copy(part[1], gres[:, 0]).then_inc(gp_chain, 1)
                pool.wait_ge(gp_chain, base + 3)
                pool.tensor_tensor(part[2], gres[:, 0], part[1], ALU.subtract).then_inc(gp_chain, 1)

            def post(c):
                pool.wait_ge(mv2_done, c + 1)
                pool.sem_inc(pool_passed, 1)
                pool.tensor_scalar(vare2[:], mv2[:, 1:2], EPS, None, ALU.add).then_inc(ve2_done, 1)
                pool.wait_ge(ve2_done, c + 1)
                pool.tensor_tensor(rstd2[:], vare2[:], expo_ln[:, 0:1], ALU.pow).then_inc(rstd2_done, 1)
                pool.tensor_copy(hres[:, bass.ds(c * DM, DM)], h2[:]).then_inc(h2_stored, 1)

            def copy_states(c):
                pool.wait_ge(h_full, CH * (c + 1))
                pool.sem_inc(pool_passed, 1)
                pool.tensor_copy(hchunk[:].rearrange("p k t b -> p t k b"),
                                 hseq[:, :, :, 1].rearrange("p t (k b) -> p t k b", k=KH)
                                 ).then_inc(hchunk_done, 1)

            def result(c, first):
                pool.wait_ge(tanho_done, c + 1)
                pool.sem_inc(pool_passed, 1)
                pool.tensor_scalar(sig_o[:], tanh_o[:], 0.5, 0.5, ALU.mult, ALU.add).then_inc(sigo_done, 1)
                if not first:
                    pool.wait_ge(out_dma, 16 * c)
                pool.wait_ge(sigo_done, c + 1)
                pool.sem_inc(pool_passed, 1)
                pool.tensor_tensor(res[:], sig_o[:], hres[:, bass.ds(c * DM, DM)],
                                   ALU.add).then_inc(res_done, 1)

            def body(c, first, last, first_store=False):
                if not first:
                    copy_states(c - 1)
                    pool.wait_ge(c_psum, CH * c)
                for g in range(3):
                    split(c, 1, g)
                if not last:
                    post(c + 1)
                if not first:
                    result(c - 1, first_store)
                if not last:
                    for g in range(3):
                        split(c + 1, 0, g)

            post(0)
            for g in range(3):
                split(0, 0, g)
            body(0, True, False)
            body(1, False, False, True)
            with pool.Fori(2, NCH - 1) as c:
                body(c, False, False)
            body(NCH - 1, False, True)
            copy_states(NCH - 1)
            result(NCH - 1, False)

        @block.scalar
        def _(act):
            a = nc.scalar
            act.dma_start(dtrow[:], log_dt.rearrange("(a d) -> a d", a=1)).then_inc(ssm_in, 16)
            act.dma_start(A_sb[:], A).then_inc(ssm_in, 16)
            act.dma_start(B_sb[:], Bm).then_inc(ssm_in, 16)
            act.dma_start(C_sb[:], C).then_inc(ssm_in, 16)
            act.dma_start(Dcol[:], D.rearrange("(d a) -> d a", a=1)).then_inc(ssm_in, 16)
            act.dma_start(Wout_sb[:], W_out).then_inc(ssm_in, 16)
            for i, v in enumerate((b2, b_out, bo)):
                act.dma_start(vec_rows[:, i, :], v.rearrange("(a d) -> a d", a=1)).then_inc(ssm_in, 16)
            act.wait_ge(ssm_in, 16 * 9)
            a.activation(dtrow[:], dtrow[:], ACT.Exp).then_inc(su_act, 1)

            for g in range(NP):
                if g:
                    act.wait_ge(spec_psum, g)
                for k in range(2):
                    act.wait_ge(patT_psum, 2 * g + k + 1)
                    a.activation(patT[:, k, :], ps_patT[:, k, 0:PT], ACT.Copy).then_inc(patT_copied, 1)
                act.wait_ge(spec_psum, g + 1)
                if g:
                    act.wait_ge(sp_dve, 2 * g)
                v = absre[:].rearrange("p (h w) -> p h w", h=2)
                a.activation(v, ps_re, ACT.Abs).then_inc(absre_done, 1)
                act.wait_ge(absre_done, g + 1)
                a.activation(re2[:], absre[:], ACT.Square).then_inc(sp_act, 1)
                act.wait_ge(im_read, g + 1)
                a.activation(im2[:], imag[:, g, :], ACT.Square).then_inc(sp_act, 1)
                a.activation(absim[:, g, :], imag[:, g, :], ACT.Abs).then_inc(sp_act, 1)
                act.wait_ge(sp_dve, 2 * g + 1)
                a.activation(group_order(magT, g)[:, :, 0], tile_order(power[:])[:, :, 0], ACT.Sqrt)
                a.activation(group_order(magT, g)[:, :, 1], tile_order(power[:])[:, :, 1],
                             ACT.Sqrt).then_inc(sp_act, 1)
            for g in range(NP):
                atan(act, a, g)

            act.wait_ge(su_pe, 3)
            a.activation(dtcol[:], ps_misc[:, 0:1], ACT.Copy, scale=1.0 / DM).then_inc(su_act, 1)
            for q in range(GQ):
                a.activation(b2_bc[:, q, :], ps_out[:, 0:DM], ACT.Copy)
                last = a.activation(bout_bc[:, q, :], ps_out[:, DM:2 * DM], ACT.Copy)
            last.then_inc(su_act, 1)
            a.activation(bo_bc[:], ps_out[:, 2 * DM:3 * DM], ACT.Copy).then_inc(su_act, 1)
            a.activation(biasT[:], ps_xT[:, 0:32], ACT.Copy).then_inc(su_act, 1)
            a.activation(WoutT[:], ps_y0[:, 0:128], ACT.Copy).then_inc(su_act, 1)
            for g in range(3):
                act.wait_ge(su_pe, 4 + g)
                a.activation(wT[:, g, :], bank(g), ACT.Copy, scale=0.5 if g == 2 else 1.0).then_inc(wT_done, 1)
            act.wait_ge(su_pe, 7)
            a.activation(WuT[:, 0:4, :].rearrange("p a d -> p (a d)"), bank(5), ACT.Copy).then_inc(wT_done, 1)
            a.activation(WuT[:, 4:6, :].rearrange("p a d -> p (a d)"), ps[:, 6, 0:256],
                         ACT.Copy).then_inc(wT_done, 1)
            a.activation(WoT[:].rearrange("p a d -> p (a d)"), ps[:, 6, 256:512], ACT.Copy).then_inc(wT_done, 1)
            act.wait_ge(su_pe, 8)
            a.activation(WCT[:], ps[0:N, 7, 128:256], ACT.Copy).then_inc(su_act, 1)

            def newton(q, kind):
                if kind == 0:
                    act.wait_ge(nt_psum, q + 1)
                    a.activation(Dn[0:N, :], ps_nt, ACT.Copy).then_inc(dn_done, 1)
                else:
                    act.wait_ge(nx_psum, q + 1)
                    a.activation(XY[0:N].rearrange("p a n -> p (a n)"), ps_nx, ACT.Copy).then_inc(xy_done, 1)

            def copy_xT(n, first):
                act.wait_ge(xT_psum, n + 1)
                if not first:
                    act.wait_ge(xT_stored, n)
                a.activation(xlnT_g[:], ps_xT, ACT.Copy).then_inc(xT_copied, 1)

            def tok(n, tail):
                for m in range(MC):
                    if SLOTS[3 * m]:
                        newton(n * NEWTON_PER_GROUP + SLOTS[3 * m][0], SLOTS[3 * m][1])
                    act.wait_ge(hid_psum, MC * n + m + 1)
                    k = msize(m)
                    a.activation(hid[0:k, m % 2, :], bank(m % 2, k), ACT.Gelu,
                                 bias=biasT[0:k, m:m + 1]).then_inc(gelu_done, 1)
                    for s in (1, 2):
                        if SLOTS[3 * m + s]:
                            newton(n * NEWTON_PER_GROUP + SLOTS[3 * m + s][0], SLOTS[3 * m + s][1])
                    if tail and m == 3:
                        copy_xT(n - 1, tail == "first")

            tok(0, None)
            tok(1, "first")
            with act.Fori(2, NG) as n:
                tok(n, "yes")
            copy_xT(NG - 1, False)

            def ssm_tanh(c, k):
                act.wait_ge(s_psum, CH * c + k + 1)
                a.activation(states[0:N, k * NB:(k + 1) * NB], ps_s[:, k * NB:(k + 1) * NB],
                             ACT.Tanh).then_inc(s_done, 1)

            def copy_x2T(c):
                act.wait_ge(x2T_psum, c + 1)
                a.activation(x2T[:], ps_p, ACT.Copy).then_inc(x2T_done, 1)

            def copy_gin(c, g, first):
                act.wait_ge(gx_psum, 3 * c + g + 1)
                if not first and g == 0:
                    act.wait_ge(gp_chain, 24 * c)
                for m in range(KH):
                    a.activation(gin[:, :, g, gate_cols(m)],
                                 ps_x[:, m * CT:(m + 1) * CT].rearrange("p (t b) -> p t b", b=NB),
                                 ACT.Identity, bias=gbias[:, KH * g + m:KH * g + m + 1]).then_inc(gin_done, 1)

            for k in range(CH):
                ssm_tanh(0, k)
            copy_x2T(0)
            for g in range(3):
                copy_gin(0, g, True)

            def body(c, first, last):
                for j in range(CH):
                    t = CH * c + j
                    act.wait_ge(r_psum, t + 1)
                    a.activation(tanh_r[:], ps_gate[0], ACT.Tanh, scale=0.5).then_inc(r_done, 1)
                    if not last and j < CH // 2:
                        ssm_tanh(c + 1, 2 * j)
                    act.wait_ge(z_psum, t + 1)
                    a.activation(tanh_z[:], ps_gate[1], ACT.Tanh, scale=0.5).then_inc(z_done, 1)
                    if not last and j == 12:
                        copy_x2T(c + 1)
                    if not last and j in (13, 14, 15):
                        copy_gin(c + 1, j - 13, False)
                    if not first and j == 11:
                        act.wait_ge(logit_done, c)
                        a.activation(tanh_o[:], logit[:], ACT.Tanh, scale=0.5).then_inc(tanho_done, 1)
                    act.wait_ge(c_psum, t + 1)
                    a.activation(addend[:, :, 0], ps_gate[2], ACT.Tanh).then_inc(c_done, 1)
                    if not last and j < CH // 2:
                        ssm_tanh(c + 1, 2 * j + 1)

            body(0, True, False)
            with act.Fori(1, NCH - 1) as c:
                body(c, False, False)
            body(NCH - 1, False, True)
            act.wait_ge(logit_done, NCH)
            a.activation(tanh_o[:], logit[:], ACT.Tanh, scale=0.5).then_inc(tanho_done, 1)

        @block.vector
        def _(dve):
            v = nc.vector
            dve.wait_ge(su_act, 1)
            v.tensor_scalar(dtrow[:], dtrow[:], 1e-4, 1.0, ALU.max, ALU.min).then_inc(su_dve, 1)
            dve.wait_ge(su_dve, 1)
            v.reduce_sum(dtsum[:], dtrow[:], AX).then_inc(su_dve, 1)
            v.transpose(AT[:], A_sb[:]).then_inc(su_dve, 1)

            for g in range(NP):
                dve.wait_ge(spec_psum, g + 1)
                w = imag[:, g, :].rearrange("p (h w) -> p h w", h=2)
                v.tensor_scalar(w, ps_im, 0.0, None, ALU.add).then_inc(im_read, 1)
                dve.wait_ge(absre_done, g + 1)
                w = neghalf[:, g, :].rearrange("p (h w) -> p h w", h=2)
                v.tensor_scalar(w, ps_re, 0.0, HALF_PI, ALU.is_lt, ALU.mult).then_inc(re_read, 1)
                dve.wait_ge(sp_act, 4 * g + 2)
                if g:
                    dve.wait_ge(sp_act, 4 * g)
                v.scalar_tensor_tensor(out=power[:], in0=re2[:], scalar=TINY_POWER, in1=im2[:],
                                       op0=ALU.max, op1=ALU.add).then_inc(sp_dve, 1)
                dve.wait_ge(sp_act, 4 * g + 4)
                denom_add(v, g)
                if g:
                    dve.wait_ge(tang_done, g)
                dve.wait_ge(sp_dve, 2 * g + 2)
                v.reciprocal(rdenom[:], denom[:]).then_inc(rden_done, 1)
            for g in range(NP):
                angle(dve, v, g)

            dve.wait_ge(su_act, 2)
            v.tensor_scalar(negdt[:], dtcol[:], -0.5, None, ALU.mult).then_inc(su_dve, 1)
            dve.wait_ge(su_dve, 4)
            dve.wait_ge(bf_ident, 3)
            dve.wait_ge(consts, 14)
            for i, s in enumerate((AT, A_sb)):
                v.scalar_tensor_tensor(out=Mt[:, i, :], in0=s[:], scalar=negdt[0:N, :], in1=eye[0:N, :],
                                       op0=ALU.mult, op1=ALU.add).then_inc(su_dve, 1)
            dve.wait_ge(su_dve, 6)
            v.tensor_tensor(sq[:], Mt[:, 0, :], Mt[:, 0, :], ALU.mult).then_inc(su_dve, 1)
            v.tensor_scalar(negMT[0:N, :], Mt[:, 0, :], -1.0, None, ALU.mult).then_inc(su_dve, 1)
            dve.wait_ge(su_dve, 8)
            v.reduce_sum(sqsum[:], sq[:], AX).then_inc(su_dve, 1)
            dve.wait_ge(su_pe, 9)
            v.reciprocal(scale0[:], ps[0:N, 7, 256:257]).then_inc(su_dve, 1)
            dve.wait_ge(su_dve, 10)
            v.tensor_scalar(XY[0:N].rearrange("p a n -> p (a n)"), Mt[:].rearrange("p a n -> p (a n)"),
                            scale0[:, 0:1], None, ALU.mult).then_inc(su_dve, 1)
            dve.wait_ge(su_act, 6)
            v.tensor_tensor(gbias[:], biasT[:, MC:MC + 3 * KH], biasT[:, MC + 3 * KH:MC + 6 * KH],
                            ALU.add).then_inc(su_dve, 1)
            v.tensor_scalar(WDT[:], WoutT[:], Dcol[:, 0:1], None, ALU.mult).then_inc(su_dve, 1)

            def tok_tail(n):
                dve.wait_ge(y0_psum, n + 1)
                dve.wait_ge(h1b_done, n + 1)
                v.tensor_tensor(hres[:, bass.ds(n * GT, GT)], ps_y0, h1b[:], ALU.add).then_inc(y0_read, 1)

            def tok_head(n, first):
                dve.wait_ge(out_psum, n + 1)
                if not first:
                    dve.wait_ge(h1b_done, n)
                v.tensor_tensor(h1[:], ps_out, b2_bc[:].rearrange("p q d -> p (q d)"),
                                ALU.add).then_inc(out_read, 1)
                dve.wait_ge(out_read, n + 1)
                for q in range(GQ):
                    v.bn_stats(stats[:, q, :], h1[:, q * DM:(q + 1) * DM]).then_inc(st_done, 1)
                dve.wait_ge(st_done, GQ * n + GQ)
                dve.sem_inc(dve_passed, 1)
                for q in range(GQ):
                    last = v.bn_aggr(mv[:, q, :], stats[:, q, :])
                last.then_inc(mv_done, 1)
                dve.wait_ge(rstd_done, n + 1)
                for q in range(GQ):
                    last = v.tensor_scalar(xln[:, q * DM:(q + 1) * DM], h1[:, q * DM:(q + 1) * DM],
                                           mv[:, q, 0:1], rstd[:, q:q + 1], ALU.subtract, ALU.mult)
                last.then_inc(xln_done, 1)

            dve.wait_ge(tok_in, 48)
            v.tensor_scalar(W1_sb[:, 1, :], W1_sb[:, 1, :], 2.0, None, ALU.mult).then_inc(su_dve, 1)
            tok_head(0, True)
            with dve.Fori(1, NG) as n:
                tok_tail(n - 1)
                tok_head(n, False)
            tok_tail(NG - 1)

            dve.wait_ge(xy_done, NG * NEWTON_PER_GROUP)
            v.scalar_tensor_tensor(out=AbarT[0:N, :], in0=XY[0:N, 1, :], scalar=2.0, in1=eye[0:N, :],
                                   op0=ALU.mult, op1=ALU.subtract).then_inc(bar_done, 1)
            dve.wait_ge(su_pe, 10)
            v.tensor_scalar(BbarT[:], ps_misc[:, 0:N], dtcol[:, 0:1], None, ALU.mult).then_inc(bar_done, 1)

            def post_a(c, first):
                dve.wait_ge(p_psum, c + 1)
                if not first:
                    dve.wait_ge(h2_stored, c)
                v.tensor_tensor(h2[:], ps_p, hres[:, bass.ds(c * DM, DM)], ALU.add).then_inc(h2_done, 1)
                dve.wait_ge(h2_done, c + 1)
                v.bn_stats(stats2[:], h2[:]).then_inc(st2_done, 1)

            def post_b(c):
                dve.wait_ge(st2_done, c + 1)
                dve.sem_inc(dve_passed, 1)
                v.bn_aggr(mv2[:], stats2[:]).then_inc(mv2_done, 1)

            def post_c(c):
                dve.wait_ge(rstd2_done, c + 1)
                v.tensor_scalar(x2[:], h2[:], mv2[:, 0:1], rstd2[:, 0:1], ALU.subtract,
                                ALU.mult).then_inc(x2_done, 1)

            post_a(0, True)
            post_b(0)
            post_c(0)

            def body(c, first, last):
                for j in range(CH):
                    t = CH * c + j
                    h_prev = hseq[:, (j - 1) % CH, :, 1]
                    dve.wait_ge(r_done, t + 1)
                    v.scalar_tensor_tensor(out=rh_hi[:], in0=tanh_r[:], scalar=1.0, in1=h_prev,
                                           op0=ALU.add, op1=ALU.mult).then_inc(rh_hi_done, 1)
                    v.scalar_tensor_tensor(out=rh[:], in0=tanh_r[:], scalar=1.0, in1=h_prev,
                                           op0=ALU.add, op1=ALU.mult).then_inc(rh_full, 1)
                    dve.wait_ge(rh_full, t + 1)
                    v.tensor_tensor(rh_lo[:], rh[:], rh_hi[:], ALU.subtract).then_inc(rh_lo_done, 1)
                    dve.wait_ge(z_done, t + 1)
                    v.tensor_scalar(zgate[:], tanh_z[:], 0.5, 0.5, ALU.mult, ALU.add).then_inc(zg_done, 1)
                    v.tensor_scalar(coef[:, :, 1], tanh_z[:], -0.5, 0.5, ALU.mult, ALU.add).then_inc(zh_done, 1)
                    dve.wait_ge(zg_done, t + 1)
                    v.tensor_tensor(addend[:, :, 1], zgate[:], h_prev, ALU.mult).then_inc(zh_done, 1)
                    if not last:
                        if j == 8:
                            post_a(c + 1, False)
                        if j == 9:
                            post_b(c + 1)
                        if j == 10:
                            post_c(c + 1)
                    if not first and j == 11:
                        dve.wait_ge(o_psum, c)
                        v.tensor_tensor(logit[:], ps_o, bo_bc[:], ALU.add).then_inc(logit_done, 1)
                    dve.wait_ge(zh_done, 2 * t + 2)
                    dve.wait_ge(c_done, t + 1)
                    scan(v, h_hi[:].rearrange("p s i -> p (s i)")).then_inc(h_hi_done, 1)
                    if not first and j == 0:
                        dve.wait_ge(hchunk_done, c)
                    scan(v, hseq[:, j].rearrange("p s i -> p (s i)")).then_inc(h_full, 1)
                    dve.wait_ge(h_full, t + 1)
                    v.tensor_tensor(h_lo[:], hseq[:, j, :, 1], h_hi[:, :, 1],
                                    ALU.subtract).then_inc(h_lo_done, 1)

            body(0, True, False)
            with dve.Fori(1, NCH - 1) as c:
                body(c, False, False)
            body(NCH - 1, False, True)
            dve.wait_ge(o_psum, NCH)
            v.tensor_tensor(logit[:], ps_o, bo_bc[:], ALU.add).then_inc(logit_done, 1)

        @block.tensor
        def _(pe):
            mm, tr = nc.tensor.matmul, nc.tensor.transpose
            pe.wait_ge(consts, 1)
            for g in range(NP):
                pe.wait_ge(x_in[g], 16)
                if g:
                    pe.wait_ge(patT_copied, 2 * g)
                for k in range(2):
                    for s in range(NS):
                        n0 = s * PATCH + k * KP
                        last = tr(ps_patT[:, k, s * 128:(s + 1) * 128], x_sb[:, g, n0:n0 + KP], ident[:])
                    last.then_inc(patT_psum, 1)
                if g == 0:
                    pe.wait_ge(dft_in, 16)
                else:
                    pe.wait_ge(re_read, g)
                    pe.wait_ge(im_read, g)
                pe.wait_ge(patT_copied, 2 * g + 2)
                for part, dst in ((0, ps_re), (1, ps_im)):
                    for hh in range(2):
                        for k in range(2):
                            last = mm(dst[:, hh], dft_sb[:, k, part, :], patT[:, k, hh * HT:(hh + 1) * HT],
                                      start=k == 0, stop=k == 1)
                last.then_inc(spec_psum, 1)

            pe.wait_ge(consts, 14)
            pe.wait_ge(su_dve, 2)
            pe.wait_ge(re_read, NP)
            pe.wait_ge(im_read, NP)
            mm(ps_misc[:, 0:1], ones_row[:], dtsum[:], start=True, stop=True).then_inc(su_pe, 1)
            mm(ps_out[:, 0:3 * DM], ones_row[:], vec_rows[:].rearrange("p a d -> p (a d)"),
               start=True, stop=True).then_inc(su_pe, 1)
            pe.wait_ge(rows_in, 16 * 8)
            tr(ps_xT[:, 0:32], bias_rows[:], ident[0:32, 0:32])
            tr(ps_y0[:, 0:128], Wout_sb[:], ident[:]).then_inc(su_pe, 1)
            pe.wait_ge(gru_in, 16 * 7)
            pe.wait_ge(su_act, 6)
            for g in range(3):
                for k in range(KH):
                    for m in range(KH):
                        last = tr(bank(g)[:, k * H + m * 128:k * H + (m + 1) * 128],
                                  wnat[:, g, m, k * 128:(k + 1) * 128], ident[:])
                last.then_inc(su_pe, 1)
            for i in range(6):
                dst = ps[:, 5 + i // 4, (i % 4) * 128:(i % 4 + 1) * 128]
                tr(dst, wunat[:, i // 2, i % 2, :], ident[:])
            for k in range(KH):
                last = tr(ps[:, 6, 256 + k * 128:384 + k * 128], wonat[:, k * 128:(k + 1) * 128], ident[:])
            last.then_inc(su_pe, 1)
            mm(ps[0:N, 7, 128:256], C_sb[:], WoutT[:], start=True, stop=True).then_inc(su_pe, 1)
            pe.wait_ge(su_dve, 9)
            pe.wait_ge(su_act, 7)
            mm(ps[0:N, 7, 256:257], ones_sq[:], sqsum[:], start=True, stop=True).then_inc(su_pe, 1)
            pe.wait_ge(su_dve, 14)
            pe.wait_ge(wT_done, 6)
            pe.wait_ge(ang_done, NP)

            def newton(q, kind, first):
                if kind == 0:
                    if not first:
                        pe.wait_ge(xy_done, q)
                    mm(ps_nt, eye2[:], eye[:], start=True, stop=False)
                    mm(ps_nt, negMT[:], XY[:, 0, :], start=False, stop=True).then_inc(nt_psum, 1)
                else:
                    pe.wait_ge(dn_done, q + 1)
                    mm(ps_nx[:, 0:N], XY[:, 1, :], Dn[:], start=True, stop=True)
                    mm(ps_nx[:, N:2 * N], Dn[:], XY[:, 1, :], start=True, stop=True).then_inc(nx_psum, 1)

            def tok(n, tail, first):
                def slot(i):
                    if SLOTS[i]:
                        newton(n * NEWTON_PER_GROUP + SLOTS[i][0], SLOTS[i][1], first and i == 0)

                def down(m, qs):
                    for q in qs:
                        k = msize(m)
                        last = mm(ps_out[:, q * DM:(q + 1) * DM], hid[0:k, m % 2, q * 128:(q + 1) * 128],
                                  W2_sb[0:k, m, :], start=(m == 0 and q == 0), stop=(m == MC - 1),
                                  skip_group_check=True)
                    return last

                for m in range(MC):
                    k = msize(m)
                    mm(bank(m % 2, k), W1_sb[:, 0, m * 128:m * 128 + k], magT[:, bass.ds(n * GT, GT)],
                       start=True, stop=False)
                    slot(3 * m)
                    mm(bank(m % 2, k), W1_sb[:, 1, m * 128:m * 128 + k], angT[:, bass.ds(n * GT, GT)],
                       start=False, stop=True).then_inc(hid_psum, 1)
                    slot(3 * m + 1)
                    if m:
                        if m == 1 and not first:
                            pe.wait_ge(out_read, n)
                        pe.wait_ge(gelu_done, MC * n + m)
                        down(m - 1, (0, 1))
                        slot(3 * m + 2)
                        down(m - 1, (2, 3))
                    else:
                        slot(3 * m + 2)
                    if tail and m == 3:
                        transpose_x(n - 1)
                    if tail and m == 5:
                        skip(n - 1, tail == "first")
                pe.wait_ge(gelu_done, MC * n + MC)
                down(MC - 1, (0, 1, 2, 3)).then_inc(out_psum, 1)

            def transpose_x(n):
                pe.wait_ge(xln_done, n + 1)
                for q in range(GQ):
                    last = tr(ps_xT[:, q * 128:(q + 1) * 128], xln[:, q * 128:(q + 1) * 128], ident[:])
                last.then_inc(xT_psum, 1)

            def skip(n, first):
                pe.wait_ge(xT_copied, n + 1)
                if not first:
                    pe.wait_ge(y0_read, n)
                for q in range(GQ):
                    last = mm(ps_y0[:, q * DM:(q + 1) * DM], xlnT_g[:, q * 128:(q + 1) * 128], WDT[:],
                              start=(q == 0), stop=(q == GQ - 1), skip_group_check=True)
                last.then_inc(y0_psum, 1)

            tok(0, None, True)
            tok(1, "first", False)
            with pe.Fori(2, NG) as n:
                tok(n, "yes", False)
            transpose_x(NG - 1)
            skip(NG - 1, False)
            pe.wait_ge(xy_done, NG * NEWTON_PER_GROUP)
            mm(ps_misc[:, 0:N], B_sb[:], XY[0:N, 1, :], start=True, stop=True).then_inc(su_pe, 1)

            def ssm_input(c):
                mm(ps_s, BbarT[:], xlnT[:, bass.ds(c * CT, CT)], start=True, stop=False, skip_group_check=True)

            def ssm_step(c, k, first=False):
                if not first:
                    pe.wait_ge(s_done, CH * c + k)
                k0 = (k - 1) % CH
                mm(ps_s[:, k * NB:(k + 1) * NB], AbarT[:], states[:, k0 * NB:(k0 + 1) * NB],
                   start=False, stop=(k == CH - 1), skip_group_check=True).then_inc(s_psum, 1)

            def ssm_out(c):
                pe.wait_ge(s_done, CH * (c + 1))
                mm(ps_p, states[0:N, :], WCT[:], start=True, stop=True).then_inc(p_psum, 1)

            def transpose_x2(c):
                pe.wait_ge(x2_done, c + 1)
                tr(ps_p, x2[:], ident[:]).then_inc(x2T_psum, 1)

            def gate_inputs(c, g, first):
                if g == 0:
                    pe.wait_ge(x2T_done, c + 1)
                if not (first and g == 0):
                    pe.wait_ge(gin_done, 6 * c + 2 * g)
                for m in range(KH):
                    last = mm(ps_x[:, m * CT:(m + 1) * CT], WuT[:, KH * g + m, :], x2T[:],
                              start=(m == 0), stop=(m == KH - 1), skip_group_check=True)
                last.then_inc(gx_psum, 1)

            def place_inputs(c, j, g):
                if j % (CH // 2) == 0:
                    pe.wait_ge(gp_chain, 24 * c + 12 * (j // (CH // 2)) + 4 * g + 4)
                for i in range(3):
                    mm(ps_gate[g], ident_bf[:], gparts[:, i, j, g, :], start=(i == 0), stop=False,
                       skip_group_check=True)

            def recur(g, state, parts, stop):
                for m in range(KH):
                    for k in range(KH):
                        for i in range(parts):
                            last = mm(ps_gate[g][:, gate_cols(m)], wparts[:, i, g, k, m * 128:(m + 1) * 128],
                                      state[:, k * NB:(k + 1) * NB], start=False,
                                      stop=stop and (m, k, i) == (KH - 1, KH - 1, parts - 1),
                                      skip_group_check=True)
                return last

            def output_product(c):
                pe.wait_ge(hchunk_done, c + 1)
                for k in range(KH):
                    last = mm(ps_o, hchunk[:, k].rearrange("p t b -> p (t b)"), WoT[:, k, :],
                              start=(k == 0), stop=(k == KH - 1))
                last.then_inc(o_psum, 1)

            pe.wait_ge(bar_done, 2)
            ssm_input(0)
            for k in range(CH):
                ssm_step(0, k, k == 0)
            ssm_out(0)
            ssm_input(1)
            transpose_x2(0)
            for g in range(3):
                gate_inputs(0, g, True)
            pe.wait_ge(wp_done, 12)
            place_inputs(0, 0, 0)
            place_inputs(0, 0, 1)

            def body(c, first, last_chunk, penultimate=False):
                for j in range(CH):
                    t = CH * c + j
                    start_of_all = first and j == 0
                    if not start_of_all:
                        pe.wait_ge(h_hi_done, t)
                    recur(0, h_hi[:, :, 1], 3, False)
                    if not start_of_all:
                        pe.wait_ge(h_lo_done, t)
                    recur(0, h_lo[:], 2, True).then_inc(r_psum, 1)
                    if not start_of_all:
                        pe.wait_ge(c_done, t)
                    place_inputs(c, j, 2)
                    if not last_chunk and j < CH // 2:
                        ssm_step(c + 1, 2 * j)
                    if not last_chunk and j == CH // 2:
                        ssm_out(c + 1)
                    recur(1, h_hi[:, :, 1], 3, False)
                    recur(1, h_lo[:], 2, True).then_inc(z_psum, 1)
                    pe.wait_ge(rh_hi_done, t + 1)
                    recur(2, rh_hi[:], 3, False)
                    pe.wait_ge(rh_lo_done, t + 1)
                    recur(2, rh_lo[:], 2, True).then_inc(c_psum, 1)
                    if not (last_chunk and j == CH - 1):
                        pe.wait_ge(r_done, t + 1)
                        pe.wait_ge(z_done, t + 1)
                        nxt = (c, j + 1) if j < CH - 1 else (c + 1, 0)
                        place_inputs(*nxt, 0)
                        place_inputs(*nxt, 1)
                    if not last_chunk:
                        if j < CH // 2:
                            ssm_step(c + 1, 2 * j + 1)
                        if j == 10:
                            transpose_x2(c + 1)
                        if j in (12, 13, 14):
                            gate_inputs(c + 1, j - 12, False)
                    if not last_chunk and not penultimate and j == 11:
                        ssm_input(c + 2)
                    if not first and j == 9:
                        output_product(c - 1)

            body(0, True, False)
            with pe.Fori(1, NCH - 2) as c:
                body(c, False, False)
            body(NCH - 2, False, False, True)
            body(NCH - 1, False, True)
            output_product(NCH - 1)


_INS = ["x", "L0_tok_W1", "L0_tok_b1", "L0_tok_W2", "L0_tok_b2", "L0_attn_A", "L0_attn_B", "L0_attn_C",
        "L0_attn_D", "L0_attn_log_dt", "L0_attn_W_out", "L0_attn_b_out", "L0_ffn_Wuz", "L0_ffn_buz",
        "L0_ffn_Wwz", "L0_ffn_bwz", "L0_ffn_Wur", "L0_ffn_bur", "L0_ffn_Wwr", "L0_ffn_bwr", "L0_ffn_Wu",
        "L0_ffn_bu", "L0_ffn_Ww", "L0_ffn_bw", "L0_ffn_Wo", "L0_ffn_bo"]
_PATCH = 200


def _dft_table():
    import numpy as np
    n = np.arange(_PATCH)[:, None]
    f = np.arange(_PATCH // 2 + 1)[None, :]
    k = (n * f) % _PATCH
    cos = np.cos(2 * np.pi * k / _PATCH)
    sin = -np.sin(2 * np.pi * k / _PATCH)
    sin[(2 * k) % _PATCH == 0] = 0.0
    both = np.stack([cos, sin], axis=1).reshape(2, _PATCH // 2, 2, _PATCH // 2 + 1)
    return np.ascontiguousarray(both.transpose(1, 0, 2, 3).astype(np.float32))


def kernel(**inputs):
    import numpy as _np
    import concourse.bacc as _bacc
    from concourse import mybir as _mybir
    from concourse.bass_utils import run_bass_kernel_spmd as _run

    nc = _bacc.Bacc("TRN2", target_bir_lowering=False, num_devices=1)
    arrays, args = {}, []
    for name in _INS:
        arrays[f"in_{name}"] = _np.ascontiguousarray(inputs[name])
    arrays["in_dft"] = _dft_table()
    for name, a in arrays.items():
        args.append(nc.dram_tensor(name, a.shape, _mybir.dt.from_np(a.dtype), kind="ExternalInput").ap())
    b, c, n = inputs["x"].shape
    shape = (b, c * (n // _PATCH), inputs["L0_tok_W2"].shape[1])
    args.append(nc.dram_tensor("out_0", shape, _mybir.dt.float32, kind="ExternalOutput").ap())
    audio_tower(nc, *args)
    r = _run(nc, [arrays], core_ids=[0])
    return r.results[0]["out_0"]
```

```python
from contextlib import ExitStack

import concourse.bass as bass
from concourse import mybir

ALU = mybir.AluOpType
ACT = mybir.ActivationFunctionType
F32 = mybir.dt.float32
BF16 = mybir.dt.bfloat16
F16 = mybir.dt.float16
U32 = mybir.dt.uint32
AX = mybir.AxisListType.X

HALF_PI = 1.5707963267948966
TINY = 1e-30
TINY_POWER = 1e-34
EPS = 1e-5
NEWTON_PER_GROUP = 10
W_SCALE = 2.0 ** 8
H_SCALE = 2.0 ** 14
G_SCALE = W_SCALE * H_SCALE
W_CLAMP = 60000.0

OUT_AT, NORM_AT, TRANSPOSE_AT, LOGIT_AT, GATES_AT = 2, 4, 5, 6, 7


def audio_tower(nc, x, W1, b1, W2, b2, A, Bm, C, D, log_dt, W_out, b_out,
                Wuz, buz, Wwz, bwz, Wur, bur, Wwr, bwr, Wu, bu, Ww, bw, Wo, bo, dft, out):
    NB, NC, LEN = x.shape
    KP = dft.shape[0]
    PATCH = 2 * KP
    NS = LEN // PATCH
    NF = PATCH // 2 + 1
    T = NC * NS
    NT = T * NB
    HID = W1.shape[1]
    DM = W2.shape[1]
    N = A.shape[0]
    H = Wwz.shape[0]
    KH = H // 128
    CH = 16
    CT = CH * NB
    NCH = T // CH
    GT = 512
    NG = NT // GT
    GQ = GT // 128
    MC = -(-HID // 128)
    ML = HID - 128 * (MC - 1)
    PAIR = 2
    NP = NB // PAIR
    PT = NS * PAIR * NC
    HT = PT // 2
    assert CT == 128 and DM == 128 and KH == 2 and PAIR * NC == 128 and HT <= 512 and H == 256

    with ExitStack() as ctx:
        def sb(name, shape, dt=F32):
            return ctx.enter_context(nc.sbuf_tensor(name, shape, dt))

        def sem(name):
            return ctx.enter_context(nc.semaphore(name))

        x_sb = sb("x_sb", [128, NP, LEN])
        dft_sb = sb("dft_sb", [KP, 2, 2, NF])
        ident = sb("ident", [128, 128])
        ident_bf = sb("ident_bf", [128, 128], BF16)
        patT = sb("patT", [KP, 2, PT])
        magT = sb("magT", [NF, NT])
        angT = sb("angT", [NF, NT])
        absre = sb("absre", [NF, PT])
        imag = sb("imag", [NF, NP, PT])
        absim = sb("absim", [NF, NP, PT])
        neghalf = sb("neghalf", [NF, NP, PT])
        re2 = sb("re2", [NF, PT])
        im2 = sb("im2", [NF, PT])
        power = sb("power", [NF, PT])
        denom = sb("denom", [NF, PT])
        rdenom = sb("rdenom", [NF, PT])
        expo_ln = sb("expo_ln", [128, GQ])
        W1_sb = sb("W1_sb", [NF, 2, HID])
        W2_sb = sb("W2_sb", [128, MC, DM])
        bias_rows = sb("bias_rows", [32, 128])
        biasT = sb("biasT", [128, 32])
        bsum = sb("bsum", [128, 3 * KH])
        gbias = sb("gbias", [128, 3 * KH])
        vec_rows = sb("vec_rows", [1, 3, DM])
        ones_row = sb("ones_row", [1, 128])
        ones_sq = sb("ones_sq", [N, N])
        b2_bc = sb("b2_bc", [128, GQ, DM])
        bout_bc = sb("bout_bc", [128, GQ, DM])
        bo_bc = sb("bo_bc", [128, DM])
        hid = sb("hid", [128, 2, GT])
        h1 = sb("h1", [128, GT])
        h1b = sb("h1b", [128, GT])
        stats = sb("stats", [128, GQ, 6])
        mv = sb("mv", [128, GQ, 2])
        var_eps = sb("var_eps", [128, GQ])
        rstd = sb("rstd", [128, GQ])
        xln = sb("xln", [128, GT])
        xlnT_g = sb("xlnT_g", [128, GT])
        xlnT = sb("xlnT", [128, NT])
        hres = sb("hres", [128, NT])
        Wout_sb = sb("Wout_sb", [128, DM])
        WoutT = sb("WoutT", [128, DM])
        WDT = sb("WDT", [128, DM])
        C_sb = sb("C_sb", [DM, N])
        WCT = sb("WCT", [N, DM])
        Dcol = sb("Dcol", [DM, 1])
        A_sb = sb("A_sb", [N, N])
        AT = sb("AT", [N, N])
        B_sb = sb("B_sb", [N, DM])
        dtrow = sb("dtrow", [1, DM])
        dtsum = sb("dtsum", [1, 1])
        dtcol = sb("dtcol", [128, 1])
        negdt = sb("negdt", [128, 1])
        Mt = sb("Mt", [N, 2, N])
        sq = sb("sq", [N, N])
        sqsum = sb("sqsum", [N, 1])
        scale0 = sb("scale0", [N, 1])
        negMT = sb("negMT", [128, N])
        eye = sb("eye", [128, N])
        eye2 = sb("eye2", [128, N])
        XY = sb("XY", [128, 2, N])
        Dn = sb("Dn", [128, N])
        AbarT = sb("AbarT", [128, N])
        BbarT = sb("BbarT", [DM, N])
        states = sb("states", [128, CT])
        wnat = sb("wnat", [128, 3, KH, H])
        wunat = sb("wunat", [128, 3, KH, DM])
        wonat = sb("wonat", [DM, H])
        wT = sb("wT", [128, 3, KH * H])
        wres = sb("wres", [128, KH * H])
        w_first = sb("w_first", [128, 3, KH, H], F16)
        w_rest = sb("w_rest", [128, 2, 3, KH, H], BF16)
        WuT = sb("WuT", [128, 3 * KH, 128])
        WoT = sb("WoT", [128, KH, DM])
        h2 = sb("h2", [128, DM])
        stats2 = sb("stats2", [128, 6])
        mv2 = sb("mv2", [128, 2])
        vare2 = sb("vare2", [128, 1])
        rstd2 = sb("rstd2", [128, 1])
        x2 = sb("x2", [128, DM])
        x2T = sb("x2T", [128, CT])
        gin = sb("gin", [128, CH, 3, KH * NB])
        gparts = sb("gparts", [128, 3, CH, 3, KH * NB], BF16)
        gres = sb("gres", [128, CH // 2, KH * NB])
        SW = KH * NB
        tanh_r = sb("tanh_r", [128, SW])
        tanh_z = sb("tanh_z", [128, SW])
        zgate = sb("zgate", [128, SW])
        coef = sb("coef", [128, SW, 2])
        addend = sb("addend", [128, SW, 2])
        h_hi = sb("h_hi", [128, SW, 2], F16)
        h_lo = sb("h_lo", [128, SW], F16)
        hseq = sb("hseq", [128, CH, SW, 2])
        rh = sb("rh", [128, SW])
        rh_hi = sb("rh_hi", [128, SW], F16)
        rh_lo = sb("rh_lo", [128, SW], F16)
        hchunk = sb("hchunk", [128, KH, CH, NB])
        logit = sb("logit", [128, DM])
        tanh_o = sb("tanh_o", [128, DM])
        sig_o = sb("sig_o", [128, DM])
        res = sb("res", [128, DM])

        ps = ctx.enter_context(nc.psum_tensor("ps", [128, 8, 512], F32))

        def bank(i, p=128, w=512):
            return ps[0:p, i, 0:w]

        ps_patT = ps[0:KP, 0:4, :].rearrange("p (k b) w -> p k (b w)", k=2)
        ps_re = ps[0:NF, 4:6, 0:HT]
        ps_im = ps[0:NF, 6:8, 0:HT]
        ps_out, ps_xT, ps_y0 = bank(2), bank(3), bank(4)
        ps_nt, ps_nx = bank(5, N, N), bank(6, N, 2 * N)
        ps_misc = bank(7)
        ps_gate = [bank(g, 128, SW) for g in range(3)]
        ps_s = [bank(3, N, CT // 2), bank(7, N, CT // 2)]
        ps_p = bank(5, 128, CT)
        ps_x = [bank(4, 128, CT), ps_p]
        ps_o = bank(6, 128, DM)

        x_in = [sem(f"x_in{g}") for g in range(NP)]
        dft_in = sem("dft_in")
        tok_in = sem("tok_in")
        rows_in = sem("rows_in")
        ssm_in = sem("ssm_in")
        gru_in = sem("gru_in")
        consts = sem("consts")
        pool_passed = sem("pool_passed")
        dve_passed = sem("dve_passed")
        bf_ident = sem("bf_ident")
        patT_psum = sem("patT_psum")
        patT_copied = sem("patT_copied")
        spec_psum = sem("spec_psum")
        absre_done = sem("absre_done")
        sp_act = sem("sp_act")
        sp_dve = sem("sp_dve")
        rden_done = sem("rden_done")
        fold_done = sem("fold_done")
        re_read = sem("re_read")
        im_read = sem("im_read")
        tang_done = sem("tang_done")
        atan_done = sem("atan_done")
        sign_done = sem("sign_done")
        ang_done = sem("ang_done")
        su_act = sem("su_act")
        su_dve = sem("su_dve")
        su_pool = sem("su_pool")
        su_pe = sem("su_pe")
        wT_done = sem("wT_done")
        wp_done = sem("wp_done")
        hid_psum = sem("hid_psum")
        gelu_done = sem("gelu_done")
        out_psum = sem("out_psum")
        out_read = sem("out_read")
        st_done = sem("st_done")
        mv_done = sem("mv_done")
        ve_done = sem("ve_done")
        rstd_done = sem("rstd_done")
        xln_done = sem("xln_done")
        xT_psum = sem("xT_psum")
        xT_copied = sem("xT_copied")
        xT_stored = sem("xT_stored")
        h1b_done = sem("h1b_done")
        y0_psum = sem("y0_psum")
        y0_read = sem("y0_read")
        nt_psum = sem("nt_psum")
        dn_done = sem("dn_done")
        nx_psum = sem("nx_psum")
        xy_done = sem("xy_done")
        bar_done = sem("bar_done")
        s_psum = sem("s_psum")
        s_done = sem("s_done")
        p_psum = sem("p_psum")
        h2_done = sem("h2_done")
        st2_done = sem("st2_done")
        mv2_done = sem("mv2_done")
        h2_stored = sem("h2_stored")
        ve2_done = sem("ve2_done")
        rstd2_done = sem("rstd2_done")
        x2_done = sem("x2_done")
        x2T_psum = sem("x2T_psum")
        x2T_done = sem("x2T_done")
        gx_psum = sem("gx_psum")
        gin_done = sem("gin_done")
        gp_chain = sem("gp_chain")
        h_hi_done = sem("h_hi_done")
        h_full = sem("h_full")
        h_lo_done = sem("h_lo_done")
        r_psum = sem("r_psum")
        z_psum = sem("z_psum")
        c_psum = sem("c_psum")
        r_done = sem("r_done")
        z_done = sem("z_done")
        c_done = sem("c_done")
        rh_hi_done = sem("rh_hi_done")
        rh_full = sem("rh_full")
        rh_lo_done = sem("rh_lo_done")
        zg_done = sem("zg_done")
        zh_done = sem("zh_done")
        hchunk_done = sem("hchunk_done")
        o_psum = sem("o_psum")
        logit_done = sem("logit_done")
        tanho_done = sem("tanho_done")
        sigo_done = sem("sigo_done")
        res_done = sem("res_done")
        out_dma = sem("out_dma")

        def group_order(t, g):
            v = t[:, :].rearrange("p (c s b) -> p s b c", c=NC, s=NS, b=NB)
            return v[:, :, PAIR * g:PAIR * g + PAIR, :]

        def tile_order(t):
            return t.rearrange("p (s b c) -> p s b c", s=NS, b=PAIR)

        def msize(m):
            return 128 if m < MC - 1 else ML

        def gate_cols(m):
            return slice(m * NB, (m + 1) * NB)

        def newton_slots():
            q = []
            for i in range(2 * NEWTON_PER_GROUP):
                q.append((i // 2, i % 2))
            while len(q) < 3 * MC:
                q.append(None)
            return q

        SLOTS = newton_slots()
        OUT_T = out.rearrange("b t d -> t b d")
        def atan(act, a, g):
            act.wait_ge(tang_done, g + 1)
            a.activation(absim[:, g, :], absim[:, g, :], ACT.Arctan).then_inc(atan_done, 1)

        def scan(v, dst):
            return v.tensor_tensor_scan(out=dst, data0=coef[:].rearrange("p s i -> p (s i)"),
                                        data1=addend[:].rearrange("p s i -> p (s i)"), initial=0.0,
                                        op0=ALU.mult, op1=ALU.add)

        def denom_add(v, g):
            for s in range(NS):
                last = v.scalar_tensor_tensor(
                    out=tile_order(denom[:])[:, s], in0=tile_order(absre[:])[:, s], scalar=TINY,
                    in1=group_order(magT, g)[:, s], op0=ALU.max, op1=ALU.add)
            last.then_inc(sp_dve, 1)

        def angle(dve, v, g):
            v.tensor_scalar(imag[:, g, :].bitcast(U32), imag[:, g, :].bitcast(U32), 0x80000000, None,
                            ALU.bitwise_and).then_inc(sign_done, 1)
            dve.wait_ge(sign_done, g + 1)
            dve.wait_ge(fold_done, g + 1)
            for s in range(NS):
                last = v.scalar_tensor_tensor(
                    out=group_order(angT, g)[:, s].bitcast(U32),
                    in0=tile_order(neghalf[:, g, :])[:, s].bitcast(U32), scalar=0x7fffffff,
                    in1=tile_order(imag[:, g, :])[:, s].bitcast(U32), op0=ALU.bitwise_and, op1=ALU.bitwise_or)
            last.then_inc(ang_done, 1)

        block = ctx.enter_context(nc.Block())

        @block.sync
        def _(sp):
            sp.dma_start(x_sb[:, 0, :], x[0:PAIR].rearrange("b c n -> (b c) n")).then_inc(x_in[0], 16)
            sp.dma_start(dft_sb[:], dft).then_inc(dft_in, 16)
            for g in range(1, NP):
                sp.dma_start(x_sb[:, g, :],
                             x[PAIR * g:PAIR * g + PAIR].rearrange("b c n -> (b c) n")).then_inc(x_in[g], 16)
            sp.dma_start(W1_sb[:], W1.rearrange("(k p) h -> p k h", p=NF)).then_inc(tok_in, 16)
            sp.dma_start(W2_sb[:, 0:MC - 1, :],
                         W2[0:128 * (MC - 1), :].rearrange("(m p) d -> p m d", p=128)).then_inc(tok_in, 16)
            sp.dma_start(W2_sb[0:ML, MC - 1, :], W2[128 * (MC - 1):HID, :]).then_inc(tok_in, 16)
            for g, (w, u) in enumerate(((Wwr, Wur), (Wwz, Wuz), (Ww, Wu))):
                sp.dma_start(wnat[:, g, :, :], w.rearrange("(m p) k -> p m k", p=128)).then_inc(gru_in, 16)
                sp.dma_start(wunat[:, g, :, :], u.rearrange("(m p) k -> p m k", p=128)).then_inc(gru_in, 16)
            sp.dma_start(wonat[:], Wo).then_inc(gru_in, 16)

            def store(c):
                sp.wait_ge(res_done, c + 1)
                sp.dma_start(OUT_T[bass.ds(c * CH, CH)], res[:]).then_inc(out_dma, 16)

            with sp.Fori(0, NCH) as c:
                store(c)
            sp.wait_ge(out_dma, 16 * NCH)

        @block.gpsimd
        def _(pool):
            pool.memset(ident[:], 0.0).then_inc(su_pool, 1)
            pool.memset(bias_rows[:], 0.0).then_inc(su_pool, 1)
            pool.wait_ge(su_pool, 2)
            pool.affine_select(out=ident[:], in_=ident[:], compare_op=ALU.not_equal, fill=1.0, base=0,
                               pattern=[[-1, 128]], channel_multiplier=1).then_inc(consts, 1)
            pool.dma_start(bias_rows[0:MC - 1, :],
                           b1[0:128 * (MC - 1)].rearrange("(m p) -> m p", p=128)).then_inc(rows_in, 16)
            pool.dma_start(bias_rows[MC - 1:MC, 0:ML],
                           b1[128 * (MC - 1):HID].rearrange("(m p) -> m p", m=1)).then_inc(rows_in, 16)
            for i, v in enumerate((bur, buz, bu, bwr, bwz, bw)):
                r = MC + KH * i
                pool.dma_start(bias_rows[r:r + KH, :],
                               v.rearrange("(m p) -> m p", p=128)).then_inc(rows_in, 16)
            pool.memset(ones_row[:], 1.0).then_inc(consts, 1)
            pool.memset(ones_sq[:], 1.0).then_inc(consts, 1)
            pool.memset(expo_ln[:], -0.5).then_inc(consts, 1)
            for z in (XY[:].rearrange("p a n -> p (a n)"), Dn[:], negMT[:], AbarT[:], states[:]):
                pool.memset(z, 0.0).then_inc(consts, 1)
            pool.memset(coef[:].rearrange("p a n -> p (a n)"), 0.0).then_inc(consts, 1)
            pool.memset(addend[:].rearrange("p a n -> p (a n)"), 0.0).then_inc(consts, 1)
            pool.memset(hseq[:].rearrange("p a b n -> p (a b n)"), 0.0).then_inc(consts, 1)
            pool.memset(h_hi[:].rearrange("p a n -> p (a n)"), 0.0).then_inc(consts, 1)
            pool.memset(h_lo[:], 0.0).then_inc(consts, 1)
            pool.wait_ge(consts, 1)
            pool.tensor_copy(ident_bf[:], ident[:]).then_inc(bf_ident, 1)
            pool.tensor_copy(eye[:], ident[:, 0:N]).then_inc(bf_ident, 1)
            pool.tensor_scalar(eye2[:], ident[:, 0:N], 2.0, None, ALU.mult).then_inc(bf_ident, 1)

            def fold(g):
                pool.wait_ge(atan_done, g + 1)
                pool.tensor_tensor(neghalf[:, g, :], absim[:, g, :], neghalf[:, g, :],
                                   ALU.subtract).then_inc(fold_done, 1)

            for g in range(NP):
                pool.wait_ge(rden_done, g + 1)
                pool.wait_ge(sp_act, 4 * g + 3)
                pool.tensor_tensor(absim[:, g, :], absim[:, g, :], rdenom[:], ALU.mult).then_inc(tang_done, 1)
                if g >= 1:
                    fold(g - 1)
            fold(NP - 1)

            for g in range(3):
                src = wT[:, g, :]
                part = [w.rearrange("p k h -> p (k h)") for w in (w_first[:, g], w_rest[:, 0, g], w_rest[:, 1, g])]
                pool.wait_ge(wT_done, g + 1)
                pool.tensor_scalar(part[0], src, W_CLAMP, -W_CLAMP, ALU.min, ALU.max).then_inc(wp_done, 1)
                pool.wait_ge(wp_done, 4 * g + 1)
                pool.tensor_tensor(wres[:], src, part[0], ALU.subtract).then_inc(wp_done, 1)
                pool.wait_ge(wp_done, 4 * g + 2)
                pool.tensor_copy(part[1], wres[:]).then_inc(wp_done, 1)
                pool.wait_ge(wp_done, 4 * g + 3)
                pool.tensor_tensor(part[2], wres[:], part[1], ALU.subtract).then_inc(wp_done, 1)
                pool.wait_ge(wp_done, 4 * g + 4)

            def tok_tail(n):
                pool.wait_ge(xT_copied, n + 1)
                pool.sem_inc(pool_passed, 1)
                pool.tensor_copy(xlnT[:, bass.ds(n * GT, GT)], xlnT_g[:]).then_inc(xT_stored, 1)

            def tok_head(n, first):
                if not first:
                    pool.wait_ge(y0_read, n)
                pool.wait_ge(out_read, n + 1)
                pool.tensor_tensor(h1b[:], h1[:], bout_bc[:].rearrange("p q d -> p (q d)"),
                                   ALU.add).then_inc(h1b_done, 1)
                pool.wait_ge(mv_done, n + 1)
                pool.sem_inc(pool_passed, 1)
                pool.tensor_scalar(var_eps[:], mv[:, :, 1], EPS, None, ALU.add).then_inc(ve_done, 1)
                pool.wait_ge(ve_done, n + 1)
                pool.tensor_tensor(rstd[:], var_eps[:], expo_ln[:], ALU.pow).then_inc(rstd_done, 1)

            pool.wait_ge(su_act, 5)
            tok_head(0, True)
            with pool.Fori(1, NG) as n:
                tok_tail(n - 1)
                tok_head(n, False)
            tok_tail(NG - 1)

            def split(c, half, g):
                s0 = half * (CH // 2)
                base = 24 * c + 12 * half + 4 * g
                src = gin[:, s0:s0 + CH // 2, g, :]
                part = [gparts[:, i, s0:s0 + CH // 2, g, :] for i in range(3)]
                pool.wait_ge(gin_done, 6 * c + 2 * g + 2)
                pool.sem_inc(pool_passed, 1)
                pool.tensor_copy(part[0], src).then_inc(gp_chain, 1)
                pool.wait_ge(gp_chain, base + 1)
                pool.tensor_tensor(gres[:], src, part[0], ALU.subtract).then_inc(gp_chain, 1)
                pool.wait_ge(gp_chain, base + 2)
                pool.sem_inc(pool_passed, 1)
                pool.tensor_copy(part[1], gres[:]).then_inc(gp_chain, 1)
                pool.wait_ge(gp_chain, base + 3)
                pool.tensor_tensor(part[2], gres[:], part[1], ALU.subtract).then_inc(gp_chain, 1)

            def post(c):
                pool.wait_ge(mv2_done, c + 1)
                pool.sem_inc(pool_passed, 1)
                pool.tensor_scalar(vare2[:], mv2[:, 1:2], EPS, None, ALU.add).then_inc(ve2_done, 1)
                pool.wait_ge(ve2_done, c + 1)
                pool.tensor_tensor(rstd2[:], vare2[:], expo_ln[:, 0:1], ALU.pow).then_inc(rstd2_done, 1)
                pool.tensor_copy(hres[:, bass.ds(c * DM, DM)], h2[:]).then_inc(h2_stored, 1)

            def copy_states(c, half):
                s0 = half * (CH // 2)
                pool.wait_ge(h_full, CH * c + s0 + CH // 2)
                pool.sem_inc(pool_passed, 1)
                pool.tensor_copy(hchunk[:, :, s0:s0 + CH // 2].rearrange("p k t b -> p t k b"),
                                 hseq[:, s0:s0 + CH // 2, :, 1].rearrange("p t (k b) -> p t k b", k=KH)
                                 ).then_inc(hchunk_done, 1)

            def result(c, first):
                pool.wait_ge(tanho_done, c + 1)
                pool.sem_inc(pool_passed, 1)
                pool.tensor_scalar(sig_o[:], tanh_o[:], 0.5, 0.5, ALU.mult, ALU.add).then_inc(sigo_done, 1)
                if not first:
                    pool.wait_ge(out_dma, 16 * c)
                pool.wait_ge(sigo_done, c + 1)
                pool.sem_inc(pool_passed, 1)
                pool.tensor_tensor(res[:], sig_o[:], hres[:, bass.ds(c * DM, DM)],
                                   ALU.add).then_inc(res_done, 1)

            def body(c, first, last, first_store=False):
                if not first:
                    copy_states(c - 1, 1)
                    pool.wait_ge(c_psum, CH * c)
                split(c, 1, 0)
                split(c, 1, 1)
                if not last:
                    post(c + 1)
                split(c, 1, 2)
                if not first:
                    result(c - 1, first_store)
                    pool.wait_ge(o_psum, c)
                copy_states(c, 0)
                if not last:
                    pool.wait_ge(c_psum, CH * c + CH // 2)
                    for g in range(3):
                        split(c + 1, 0, g)

            post(0)
            for g in range(3):
                split(0, 0, g)
            body(0, True, False)
            body(1, False, False, True)
            with pool.Fori(2, NCH - 1) as c:
                body(c, False, False)
            body(NCH - 1, False, True)
            copy_states(NCH - 1, 1)
            result(NCH - 1, False)

        @block.scalar
        def _(act):
            a = nc.scalar
            act.dma_start(dtrow[:], log_dt.rearrange("(a d) -> a d", a=1)).then_inc(ssm_in, 16)
            act.dma_start(A_sb[:], A).then_inc(ssm_in, 16)
            act.dma_start(B_sb[:], Bm).then_inc(ssm_in, 16)
            act.dma_start(C_sb[:], C).then_inc(ssm_in, 16)
            act.dma_start(Dcol[:], D.rearrange("(d a) -> d a", a=1)).then_inc(ssm_in, 16)
            act.dma_start(Wout_sb[:], W_out).then_inc(ssm_in, 16)
            for i, v in enumerate((b2, b_out, bo)):
                act.dma_start(vec_rows[:, i, :], v.rearrange("(a d) -> a d", a=1)).then_inc(ssm_in, 16)
            act.wait_ge(ssm_in, 16 * 9)
            a.activation(dtrow[:], dtrow[:], ACT.Exp).then_inc(su_act, 1)

            for g in range(NP):
                if g:
                    act.wait_ge(spec_psum, g)
                for k in range(2):
                    act.wait_ge(patT_psum, 2 * g + k + 1)
                    a.activation(patT[:, k, :], ps_patT[:, k, 0:PT], ACT.Copy).then_inc(patT_copied, 1)
                act.wait_ge(spec_psum, g + 1)
                if g:
                    act.wait_ge(sp_dve, 2 * g)
                v = absre[:].rearrange("p (h w) -> p h w", h=2)
                a.activation(v, ps_re, ACT.Abs).then_inc(absre_done, 1)
                act.wait_ge(absre_done, g + 1)
                a.activation(re2[:], absre[:], ACT.Square).then_inc(sp_act, 1)
                act.wait_ge(im_read, g + 1)
                a.activation(im2[:], imag[:, g, :], ACT.Square).then_inc(sp_act, 1)
                a.activation(absim[:, g, :], imag[:, g, :], ACT.Abs).then_inc(sp_act, 1)
                act.wait_ge(sp_dve, 2 * g + 1)
                a.activation(group_order(magT, g)[:, :, 0], tile_order(power[:])[:, :, 0], ACT.Sqrt)
                a.activation(group_order(magT, g)[:, :, 1], tile_order(power[:])[:, :, 1],
                             ACT.Sqrt).then_inc(sp_act, 1)
            for g in range(NP):
                atan(act, a, g)

            act.wait_ge(su_pe, 3)
            a.activation(dtcol[:], ps_misc[:, 0:1], ACT.Copy, scale=1.0 / DM).then_inc(su_act, 1)
            for q in range(GQ):
                a.activation(b2_bc[:, q, :], ps_out[:, 0:DM], ACT.Copy)
                last = a.activation(bout_bc[:, q, :], ps_out[:, DM:2 * DM], ACT.Copy)
            last.then_inc(su_act, 1)
            a.activation(bo_bc[:], ps_out[:, 2 * DM:3 * DM], ACT.Copy).then_inc(su_act, 1)
            a.activation(biasT[:], ps_xT[:, 0:32], ACT.Copy).then_inc(su_act, 1)
            a.activation(WoutT[:], ps_y0[:, 0:128], ACT.Copy).then_inc(su_act, 1)
            for g in range(3):
                act.wait_ge(su_pe, 4 + g)
                a.activation(wT[:, g, :], bank(g), ACT.Copy, scale=W_SCALE * (0.5 if g == 2 else 1.0)).then_inc(wT_done, 1)
            act.wait_ge(su_pe, 7)
            a.activation(WuT[:, 0:4, :].rearrange("p a d -> p (a d)"), bank(5), ACT.Copy,
                         scale=G_SCALE).then_inc(wT_done, 1)
            a.activation(WuT[:, 4:6, :].rearrange("p a d -> p (a d)"), ps[:, 6, 0:256],
                         ACT.Copy, scale=G_SCALE).then_inc(wT_done, 1)
            a.activation(WoT[:].rearrange("p a d -> p (a d)"), ps[:, 6, 256:512], ACT.Copy,
                         scale=1.0 / H_SCALE).then_inc(wT_done, 1)
            act.wait_ge(su_pe, 8)
            a.activation(WCT[:], ps[0:N, 7, 128:256], ACT.Copy).then_inc(su_act, 1)

            def newton(q, kind):
                if kind == 0:
                    act.wait_ge(nt_psum, q + 1)
                    a.activation(Dn[0:N, :], ps_nt, ACT.Copy).then_inc(dn_done, 1)
                else:
                    act.wait_ge(nx_psum, q + 1)
                    a.activation(XY[0:N].rearrange("p a n -> p (a n)"), ps_nx, ACT.Copy).then_inc(xy_done, 1)

            def copy_xT(n, first):
                act.wait_ge(xT_psum, n + 1)
                if not first:
                    act.wait_ge(xT_stored, n)
                a.activation(xlnT_g[:], ps_xT, ACT.Copy).then_inc(xT_copied, 1)

            def tok(n, tail):
                for m in range(MC):
                    if SLOTS[3 * m]:
                        newton(n * NEWTON_PER_GROUP + SLOTS[3 * m][0], SLOTS[3 * m][1])
                    act.wait_ge(hid_psum, MC * n + m + 1)
                    k = msize(m)
                    a.activation(hid[0:k, m % 2, :], bank(m % 2, k), ACT.Gelu,
                                 bias=biasT[0:k, m:m + 1]).then_inc(gelu_done, 1)
                    for s in (1, 2):
                        if SLOTS[3 * m + s]:
                            newton(n * NEWTON_PER_GROUP + SLOTS[3 * m + s][0], SLOTS[3 * m + s][1])
                    if tail and m == 3:
                        copy_xT(n - 1, tail == "first")

            tok(0, None)
            tok(1, "first")
            with act.Fori(2, NG) as n:
                tok(n, "yes")
            copy_xT(NG - 1, False)

            def ssm_tanh(c, k):
                act.wait_ge(s_psum, CH * c + k + 1)
                k1 = k % (CH // 2)
                a.activation(states[0:N, k * NB:(k + 1) * NB], ps_s[k // (CH // 2)][:, k1 * NB:(k1 + 1) * NB],
                             ACT.Tanh).then_inc(s_done, 1)

            def copy_x2T(c):
                act.wait_ge(x2T_psum, c + 1)
                a.activation(x2T[:], ps_p, ACT.Copy).then_inc(x2T_done, 1)

            def copy_gin(c, i, first):
                g, m = i // KH, i % KH
                act.wait_ge(gx_psum, 3 * KH * c + i + 1)
                if not first and i == 0:
                    act.wait_ge(gp_chain, 24 * c)
                a.activation(gin[:, :, g, gate_cols(m)],
                             ps_x[i % 2].rearrange("p (t b) -> p t b", b=NB),
                             ACT.Identity, bias=gbias[:, i:i + 1]).then_inc(gin_done, 1)

            for k in range(CH):
                ssm_tanh(0, k)
            copy_x2T(0)
            for i in range(3 * KH):
                copy_gin(0, i, True)
            for k in range(CH):
                ssm_tanh(1, k)
            ssm_tanh(2, 0)

            def body(c, out_before, post_next, scan_2, scan_3):
                for j in range(CH):
                    t = CH * c + j
                    act.wait_ge(r_psum, t + 1)
                    a.activation(tanh_r[:], ps_gate[0], ACT.Tanh, scale=0.5 / G_SCALE).then_inc(r_done, 1)
                    act.wait_ge(z_psum, t + 1)
                    a.activation(tanh_z[:], ps_gate[1], ACT.Tanh, scale=0.5 / G_SCALE).then_inc(z_done, 1)
                    if scan_2 and j < CH - 1:
                        ssm_tanh(c + 2, j + 1)
                    if scan_3 and j == CH - 1:
                        ssm_tanh(c + 3, 0)
                    act.wait_ge(c_psum, t + 1)
                    a.activation(addend[:, :, 0], ps_gate[2], ACT.Tanh, scale=1.0 / G_SCALE).then_inc(c_done, 1)
                    if post_next and j == TRANSPOSE_AT + 1:
                        copy_x2T(c + 1)
                    if post_next and 0 <= j - GATES_AT - 1 < 3 * KH:
                        copy_gin(c + 1, j - GATES_AT - 1, False)
                    if out_before and j == LOGIT_AT + 1:
                        act.wait_ge(logit_done, c)
                        a.activation(tanh_o[:], logit[:], ACT.Tanh, scale=0.5).then_inc(tanho_done, 1)

            body(0, False, True, True, True)
            with act.Fori(1, NCH - 3) as c:
                body(c, True, True, True, True)
            body(NCH - 3, True, True, True, False)
            body(NCH - 2, True, True, False, False)
            body(NCH - 1, True, False, False, False)
            act.wait_ge(logit_done, NCH)
            a.activation(tanh_o[:], logit[:], ACT.Tanh, scale=0.5).then_inc(tanho_done, 1)

        @block.vector
        def _(dve):
            v = nc.vector
            dve.wait_ge(su_act, 1)
            v.tensor_scalar(dtrow[:], dtrow[:], 1e-4, 1.0, ALU.max, ALU.min).then_inc(su_dve, 1)
            dve.wait_ge(su_dve, 1)
            v.reduce_sum(dtsum[:], dtrow[:], AX).then_inc(su_dve, 1)
            v.transpose(AT[:], A_sb[:]).then_inc(su_dve, 1)

            for g in range(NP):
                dve.wait_ge(spec_psum, g + 1)
                w = imag[:, g, :].rearrange("p (h w) -> p h w", h=2)
                v.tensor_scalar(w, ps_im, 0.0, None, ALU.add).then_inc(im_read, 1)
                dve.wait_ge(absre_done, g + 1)
                w = neghalf[:, g, :].rearrange("p (h w) -> p h w", h=2)
                v.tensor_scalar(w, ps_re, 0.0, HALF_PI, ALU.is_lt, ALU.mult).then_inc(re_read, 1)
                dve.wait_ge(sp_act, 4 * g + 2)
                if g:
                    dve.wait_ge(sp_act, 4 * g)
                v.scalar_tensor_tensor(out=power[:], in0=re2[:], scalar=TINY_POWER, in1=im2[:],
                                       op0=ALU.max, op1=ALU.add).then_inc(sp_dve, 1)
                dve.wait_ge(sp_act, 4 * g + 4)
                denom_add(v, g)
                if g:
                    dve.wait_ge(tang_done, g)
                dve.wait_ge(sp_dve, 2 * g + 2)
                v.reciprocal(rdenom[:], denom[:]).then_inc(rden_done, 1)
            for g in range(NP):
                angle(dve, v, g)

            dve.wait_ge(su_act, 2)
            v.tensor_scalar(negdt[:], dtcol[:], -0.5, None, ALU.mult).then_inc(su_dve, 1)
            dve.wait_ge(su_dve, 4)
            dve.wait_ge(bf_ident, 3)
            dve.wait_ge(consts, 14)
            for i, s in enumerate((AT, A_sb)):
                v.scalar_tensor_tensor(out=Mt[:, i, :], in0=s[:], scalar=negdt[0:N, :], in1=eye[0:N, :],
                                       op0=ALU.mult, op1=ALU.add).then_inc(su_dve, 1)
            dve.wait_ge(su_dve, 6)
            v.tensor_tensor(sq[:], Mt[:, 0, :], Mt[:, 0, :], ALU.mult).then_inc(su_dve, 1)
            v.tensor_scalar(negMT[0:N, :], Mt[:, 0, :], -1.0, None, ALU.mult).then_inc(su_dve, 1)
            dve.wait_ge(su_dve, 8)
            v.reduce_sum(sqsum[:], sq[:], AX).then_inc(su_dve, 1)
            dve.wait_ge(su_pe, 9)
            v.reciprocal(scale0[:], ps[0:N, 7, 256:257]).then_inc(su_dve, 1)
            dve.wait_ge(su_dve, 10)
            v.tensor_scalar(XY[0:N].rearrange("p a n -> p (a n)"), Mt[:].rearrange("p a n -> p (a n)"),
                            scale0[:, 0:1], None, ALU.mult).then_inc(su_dve, 1)
            dve.wait_ge(su_act, 6)
            v.tensor_tensor(bsum[:], biasT[:, MC:MC + 3 * KH], biasT[:, MC + 3 * KH:MC + 6 * KH],
                            ALU.add).then_inc(su_dve, 1)
            dve.wait_ge(su_dve, 12)
            v.tensor_scalar(gbias[:], bsum[:], G_SCALE, None, ALU.mult).then_inc(su_dve, 1)
            v.tensor_scalar(WDT[:], WoutT[:], Dcol[:, 0:1], None, ALU.mult).then_inc(su_dve, 1)

            def tok_tail(n):
                dve.wait_ge(y0_psum, n + 1)
                dve.wait_ge(h1b_done, n + 1)
                v.tensor_tensor(hres[:, bass.ds(n * GT, GT)], ps_y0, h1b[:], ALU.add).then_inc(y0_read, 1)

            def tok_head(n, first):
                dve.wait_ge(out_psum, n + 1)
                if not first:
                    dve.wait_ge(h1b_done, n)
                v.tensor_tensor(h1[:], ps_out, b2_bc[:].rearrange("p q d -> p (q d)"),
                                ALU.add).then_inc(out_read, 1)
                dve.wait_ge(out_read, n + 1)
                for q in range(GQ):
                    v.bn_stats(stats[:, q, :], h1[:, q * DM:(q + 1) * DM]).then_inc(st_done, 1)
                dve.wait_ge(st_done, GQ * n + GQ)
                dve.sem_inc(dve_passed, 1)
                for q in range(GQ):
                    last = v.bn_aggr(mv[:, q, :], stats[:, q, :])
                last.then_inc(mv_done, 1)
                dve.wait_ge(rstd_done, n + 1)
                for q in range(GQ):
                    last = v.tensor_scalar(xln[:, q * DM:(q + 1) * DM], h1[:, q * DM:(q + 1) * DM],
                                           mv[:, q, 0:1], rstd[:, q:q + 1], ALU.subtract, ALU.mult)
                last.then_inc(xln_done, 1)

            dve.wait_ge(tok_in, 48)
            v.tensor_scalar(W1_sb[:, 1, :], W1_sb[:, 1, :], 2.0, None, ALU.mult).then_inc(su_dve, 1)
            tok_head(0, True)
            with dve.Fori(1, NG) as n:
                tok_tail(n - 1)
                tok_head(n, False)
            tok_tail(NG - 1)

            dve.wait_ge(xy_done, NG * NEWTON_PER_GROUP)
            v.scalar_tensor_tensor(out=AbarT[0:N, :], in0=XY[0:N, 1, :], scalar=2.0, in1=eye[0:N, :],
                                   op0=ALU.mult, op1=ALU.subtract).then_inc(bar_done, 1)
            dve.wait_ge(su_pe, 10)
            v.tensor_scalar(BbarT[:], ps_misc[:, 0:N], dtcol[:, 0:1], None, ALU.mult).then_inc(bar_done, 1)

            def post_h2(c, first):
                dve.wait_ge(p_psum, c + 1)
                if not first:
                    dve.wait_ge(h2_stored, c)
                v.tensor_tensor(h2[:], ps_p, hres[:, bass.ds(c * DM, DM)], ALU.add).then_inc(h2_done, 1)

            def post_stats(c):
                dve.wait_ge(h2_done, c + 1)
                v.bn_stats(stats2[:], h2[:]).then_inc(st2_done, 1)

            def post_aggr(c):
                dve.wait_ge(st2_done, c + 1)
                dve.sem_inc(dve_passed, 1)
                v.bn_aggr(mv2[:], stats2[:]).then_inc(mv2_done, 1)

            def post_norm(c):
                dve.wait_ge(rstd2_done, c + 1)
                v.tensor_scalar(x2[:], h2[:], mv2[:, 0:1], rstd2[:, 0:1], ALU.subtract,
                                ALU.mult).then_inc(x2_done, 1)

            post_h2(0, True)
            post_stats(0)
            post_aggr(0)
            post_norm(0)

            def body(c, first, last):
                for j in range(CH):
                    t = CH * c + j
                    h_prev = hseq[:, (j - 1) % CH, :, 1]
                    dve.wait_ge(r_done, t + 1)
                    v.scalar_tensor_tensor(out=rh_hi[:], in0=tanh_r[:], scalar=1.0, in1=h_prev,
                                           op0=ALU.add, op1=ALU.mult).then_inc(rh_hi_done, 1)
                    v.scalar_tensor_tensor(out=rh[:], in0=tanh_r[:], scalar=1.0, in1=h_prev,
                                           op0=ALU.add, op1=ALU.mult).then_inc(rh_full, 1)
                    dve.wait_ge(rh_full, t + 1)
                    v.tensor_tensor(rh_lo[:], rh[:], rh_hi[:], ALU.subtract).then_inc(rh_lo_done, 1)
                    dve.wait_ge(z_done, t + 1)
                    v.tensor_scalar(zgate[:], tanh_z[:], 0.5, 0.5, ALU.mult, ALU.add).then_inc(zg_done, 1)
                    v.tensor_scalar(coef[:, :, 1], tanh_z[:], -0.5 * H_SCALE, 0.5 * H_SCALE, ALU.mult, ALU.add).then_inc(zh_done, 1)
                    dve.wait_ge(zg_done, t + 1)
                    v.tensor_tensor(addend[:, :, 1], zgate[:], h_prev, ALU.mult).then_inc(zh_done, 1)
                    dve.wait_ge(zh_done, 2 * t + 2)
                    dve.wait_ge(c_done, t + 1)
                    scan(v, h_hi[:].rearrange("p s i -> p (s i)")).then_inc(h_hi_done, 1)
                    if not first and j == 0:
                        dve.wait_ge(hchunk_done, 2 * c - 1)
                    if not first and j == CH // 2:
                        dve.wait_ge(hchunk_done, 2 * c)
                    scan(v, hseq[:, j].rearrange("p s i -> p (s i)")).then_inc(h_full, 1)
                    dve.wait_ge(h_full, t + 1)
                    v.tensor_tensor(h_lo[:], hseq[:, j, :, 1], h_hi[:, :, 1],
                                    ALU.subtract).then_inc(h_lo_done, 1)
                    if not last and j == 0:
                        post_h2(c + 1, False)
                    if not last and j == 1:
                        post_stats(c + 1)
                    if not last and j == 2:
                        post_aggr(c + 1)
                    if not last and j == NORM_AT:
                        post_norm(c + 1)
                    if not first and j == LOGIT_AT:
                        dve.wait_ge(o_psum, c)
                        v.tensor_tensor(logit[:], ps_o, bo_bc[:], ALU.add).then_inc(logit_done, 1)

            body(0, True, False)
            with dve.Fori(1, NCH - 1) as c:
                body(c, False, False)
            body(NCH - 1, False, True)
            dve.wait_ge(o_psum, NCH)
            v.tensor_tensor(logit[:], ps_o, bo_bc[:], ALU.add).then_inc(logit_done, 1)

        @block.tensor
        def _(pe):
            mm, tr = nc.tensor.matmul, nc.tensor.transpose
            pe.wait_ge(consts, 1)
            for g in range(NP):
                pe.wait_ge(x_in[g], 16)
                if g:
                    pe.wait_ge(patT_copied, 2 * g)
                for k in range(2):
                    for s in range(NS):
                        n0 = s * PATCH + k * KP
                        last = tr(ps_patT[:, k, s * 128:(s + 1) * 128], x_sb[:, g, n0:n0 + KP], ident[:])
                    last.then_inc(patT_psum, 1)
                if g == 0:
                    pe.wait_ge(dft_in, 16)
                else:
                    pe.wait_ge(re_read, g)
                    pe.wait_ge(im_read, g)
                pe.wait_ge(patT_copied, 2 * g + 2)
                for part, dst in ((0, ps_re), (1, ps_im)):
                    for hh in range(2):
                        for k in range(2):
                            last = mm(dst[:, hh], dft_sb[:, k, part, :], patT[:, k, hh * HT:(hh + 1) * HT],
                                      start=k == 0, stop=k == 1)
                last.then_inc(spec_psum, 1)

            pe.wait_ge(consts, 14)
            pe.wait_ge(su_dve, 2)
            pe.wait_ge(re_read, NP)
            pe.wait_ge(im_read, NP)
            mm(ps_misc[:, 0:1], ones_row[:], dtsum[:], start=True, stop=True).then_inc(su_pe, 1)
            mm(ps_out[:, 0:3 * DM], ones_row[:], vec_rows[:].rearrange("p a d -> p (a d)"),
               start=True, stop=True).then_inc(su_pe, 1)
            pe.wait_ge(rows_in, 16 * 8)
            tr(ps_xT[:, 0:32], bias_rows[:], ident[0:32, 0:32])
            tr(ps_y0[:, 0:128], Wout_sb[:], ident[:]).then_inc(su_pe, 1)
            pe.wait_ge(gru_in, 16 * 7)
            pe.wait_ge(su_act, 6)
            for g in range(3):
                for k in range(KH):
                    for m in range(KH):
                        last = tr(bank(g)[:, k * H + m * 128:k * H + (m + 1) * 128],
                                  wnat[:, g, m, k * 128:(k + 1) * 128], ident[:])
                last.then_inc(su_pe, 1)
            for i in range(6):
                dst = ps[:, 5 + i // 4, (i % 4) * 128:(i % 4 + 1) * 128]
                tr(dst, wunat[:, i // 2, i % 2, :], ident[:])
            for k in range(KH):
                last = tr(ps[:, 6, 256 + k * 128:384 + k * 128], wonat[:, k * 128:(k + 1) * 128], ident[:])
            last.then_inc(su_pe, 1)
            mm(ps[0:N, 7, 128:256], C_sb[:], WoutT[:], start=True, stop=True).then_inc(su_pe, 1)
            pe.wait_ge(su_dve, 9)
            pe.wait_ge(su_act, 7)
            mm(ps[0:N, 7, 256:257], ones_sq[:], sqsum[:], start=True, stop=True).then_inc(su_pe, 1)
            pe.wait_ge(su_dve, 15)
            pe.wait_ge(wT_done, 6)
            pe.wait_ge(ang_done, NP)

            def newton(q, kind, first):
                if kind == 0:
                    if not first:
                        pe.wait_ge(xy_done, q)
                    mm(ps_nt, eye2[:], eye[:], start=True, stop=False)
                    mm(ps_nt, negMT[:], XY[:, 0, :], start=False, stop=True).then_inc(nt_psum, 1)
                else:
                    pe.wait_ge(dn_done, q + 1)
                    mm(ps_nx[:, 0:N], XY[:, 1, :], Dn[:], start=True, stop=True)
                    mm(ps_nx[:, N:2 * N], Dn[:], XY[:, 1, :], start=True, stop=True).then_inc(nx_psum, 1)

            def tok(n, tail, first):
                def slot(i):
                    if SLOTS[i]:
                        newton(n * NEWTON_PER_GROUP + SLOTS[i][0], SLOTS[i][1], first and i == 0)

                def down(m, qs):
                    for q in qs:
                        k = msize(m)
                        last = mm(ps_out[:, q * DM:(q + 1) * DM], hid[0:k, m % 2, q * 128:(q + 1) * 128],
                                  W2_sb[0:k, m, :], start=(m == 0 and q == 0), stop=(m == MC - 1),
                                  skip_group_check=True)
                    return last

                for m in range(MC):
                    k = msize(m)
                    mm(bank(m % 2, k), W1_sb[:, 0, m * 128:m * 128 + k], magT[:, bass.ds(n * GT, GT)],
                       start=True, stop=False)
                    slot(3 * m)
                    mm(bank(m % 2, k), W1_sb[:, 1, m * 128:m * 128 + k], angT[:, bass.ds(n * GT, GT)],
                       start=False, stop=True).then_inc(hid_psum, 1)
                    slot(3 * m + 1)
                    if m:
                        if m == 1 and not first:
                            pe.wait_ge(out_read, n)
                        pe.wait_ge(gelu_done, MC * n + m)
                        down(m - 1, (0, 1))
                        slot(3 * m + 2)
                        down(m - 1, (2, 3))
                    else:
                        slot(3 * m + 2)
                    if tail and m == 3:
                        transpose_x(n - 1)
                    if tail and m == 5:
                        skip(n - 1, tail == "first")
                pe.wait_ge(gelu_done, MC * n + MC)
                down(MC - 1, (0, 1, 2, 3)).then_inc(out_psum, 1)

            def transpose_x(n):
                pe.wait_ge(xln_done, n + 1)
                for q in range(GQ):
                    last = tr(ps_xT[:, q * 128:(q + 1) * 128], xln[:, q * 128:(q + 1) * 128], ident[:])
                last.then_inc(xT_psum, 1)

            def skip(n, first):
                pe.wait_ge(xT_copied, n + 1)
                if not first:
                    pe.wait_ge(y0_read, n)
                for q in range(GQ):
                    last = mm(ps_y0[:, q * DM:(q + 1) * DM], xlnT_g[:, q * 128:(q + 1) * 128], WDT[:],
                              start=(q == 0), stop=(q == GQ - 1), skip_group_check=True)
                last.then_inc(y0_psum, 1)

            tok(0, None, True)
            tok(1, "first", False)
            with pe.Fori(2, NG) as n:
                tok(n, "yes", False)
            transpose_x(NG - 1)
            skip(NG - 1, False)
            pe.wait_ge(xy_done, NG * NEWTON_PER_GROUP)
            mm(ps_misc[:, 0:N], B_sb[:], XY[0:N, 1, :], start=True, stop=True).then_inc(su_pe, 1)

            def ssm_input(c, half):
                mm(ps_s[half], BbarT[:], xlnT[:, bass.ds(c * CT + half * (CT // 2), CT // 2)], start=True,
                   stop=False, skip_group_check=True)

            def ssm_step(c, k, first=False):
                if not first:
                    pe.wait_ge(s_done, CH * c + k)
                k0, k1 = (k - 1) % CH, k % (CH // 2)
                mm(ps_s[k // (CH // 2)][:, k1 * NB:(k1 + 1) * NB], AbarT[:], states[:, k0 * NB:(k0 + 1) * NB],
                   start=False, stop=(k1 == CH // 2 - 1), skip_group_check=True).then_inc(s_psum, 1)

            def ssm_out(c, first):
                pe.wait_ge(s_done, CH * (c + 1))
                if not first:
                    pe.wait_ge(gin_done, 3 * KH * c)
                mm(ps_p, states[0:N, :], WCT[:], start=True, stop=True).then_inc(p_psum, 1)

            def transpose_x2(c):
                pe.wait_ge(x2_done, c + 1)
                tr(ps_p, x2[:], ident[:]).then_inc(x2T_psum, 1)

            def gate_inputs(c, i, first):
                if i == 0:
                    pe.wait_ge(x2T_done, c + 1)
                    if not first:
                        pe.wait_ge(gin_done, 3 * KH * c)
                if i >= 2:
                    pe.wait_ge(gin_done, 3 * KH * c + i - 1)
                mm(ps_x[i % 2], WuT[:, i, :], x2T[:], start=True, stop=True).then_inc(gx_psum, 1)

            def place_inputs(c, j, g):
                if j % (CH // 2) == 0:
                    pe.wait_ge(gp_chain, 24 * c + 12 * (j // (CH // 2)) + 4 * g + 4)
                for i in range(3):
                    mm(ps_gate[g], ident_bf[:], gparts[:, i, j, g, :], start=(i == 0), stop=False,
                       skip_group_check=True)

            def recur_hi(g, state):
                for m in range(KH):
                    for k in range(KH):
                        for w in (w_first[:, g, k], w_rest[:, 0, g, k], w_rest[:, 1, g, k]):
                            mm(ps_gate[g][:, gate_cols(m)], w[:, m * 128:(m + 1) * 128],
                               state[:, k * NB:(k + 1) * NB], start=False, stop=False, skip_group_check=True)

            def recur_lo(g, state):
                for m in range(KH):
                    for k in range(KH):
                        last = mm(ps_gate[g][:, gate_cols(m)], w_first[:, g, k, m * 128:(m + 1) * 128],
                                  state[:, k * NB:(k + 1) * NB], start=False, stop=(m, k) == (KH - 1, KH - 1),
                                  skip_group_check=True)
                return last

            def output_product(c, k):
                if k == 0:
                    pe.wait_ge(hchunk_done, 2 * c + 2)
                last = mm(ps_o, hchunk[:, k].rearrange("p t b -> p (t b)"), WoT[:, k, :],
                          start=k == 0, stop=k == KH - 1)
                if k == KH - 1:
                    last.then_inc(o_psum, 1)

            pe.wait_ge(bar_done, 2)
            ssm_input(0, 0)
            ssm_input(0, 1)
            for k in range(CH):
                ssm_step(0, k, k == 0)
            ssm_out(0, True)
            ssm_input(1, 0)
            ssm_input(1, 1)
            transpose_x2(0)
            for i in range(3 * KH):
                gate_inputs(0, i, True)
            for k in range(CH):
                ssm_step(1, k)
            ssm_out(1, False)
            ssm_input(2, 0)
            ssm_input(2, 1)
            ssm_step(2, 0)
            pe.wait_ge(wp_done, 12)
            place_inputs(0, 0, 0)
            place_inputs(0, 0, 1)

            def body(c, out_before, post_next, scan_2, scan_3):
                for j in range(CH):
                    t = CH * c + j
                    start_of_all = not out_before and j == 0
                    if not start_of_all:
                        pe.wait_ge(h_hi_done, t)
                    recur_hi(0, h_hi[:, :, 1])
                    if not start_of_all:
                        pe.wait_ge(h_lo_done, t)
                    recur_lo(0, h_lo[:]).then_inc(r_psum, 1)
                    if not start_of_all:
                        pe.wait_ge(c_done, t)
                    place_inputs(c, j, 2)
                    recur_hi(1, h_hi[:, :, 1])
                    recur_lo(1, h_lo[:]).then_inc(z_psum, 1)
                    if scan_2 and j < CH - 1:
                        ssm_step(c + 2, j + 1)
                    if scan_3 and j == CH - 1:
                        ssm_step(c + 3, 0)
                    pe.wait_ge(rh_hi_done, t + 1)
                    recur_hi(2, rh_hi[:])
                    pe.wait_ge(rh_lo_done, t + 1)
                    recur_lo(2, rh_lo[:]).then_inc(c_psum, 1)
                    if post_next or j < CH - 1:
                        pe.wait_ge(r_done, t + 1)
                        pe.wait_ge(z_done, t + 1)
                        nxt = (c, j + 1) if j < CH - 1 else (c + 1, 0)
                        place_inputs(*nxt, 0)
                        place_inputs(*nxt, 1)
                    if scan_2 and out_before and j == 1:
                        ssm_input(c + 2, 1)
                    if out_before and j in (OUT_AT, OUT_AT + 1):
                        output_product(c - 1, j - OUT_AT)
                    if post_next and j == TRANSPOSE_AT:
                        transpose_x2(c + 1)
                    if post_next and 0 <= j - GATES_AT < 3 * KH:
                        gate_inputs(c + 1, j - GATES_AT, False)
                    if scan_3 and j == CH - 3:
                        ssm_input(c + 3, 0)
                    if scan_2 and j == CH - 2:
                        ssm_out(c + 2, False)

            body(0, False, True, True, True)
            with pe.Fori(1, NCH - 3) as c:
                body(c, True, True, True, True)
            body(NCH - 3, True, True, True, False)
            body(NCH - 2, True, True, False, False)
            body(NCH - 1, True, False, False, False)
            output_product(NCH - 1, 0)
            output_product(NCH - 1, 1)


_INS = ["x", "L0_tok_W1", "L0_tok_b1", "L0_tok_W2", "L0_tok_b2", "L0_attn_A", "L0_attn_B", "L0_attn_C",
        "L0_attn_D", "L0_attn_log_dt", "L0_attn_W_out", "L0_attn_b_out", "L0_ffn_Wuz", "L0_ffn_buz",
        "L0_ffn_Wwz", "L0_ffn_bwz", "L0_ffn_Wur", "L0_ffn_bur", "L0_ffn_Wwr", "L0_ffn_bwr", "L0_ffn_Wu",
        "L0_ffn_bu", "L0_ffn_Ww", "L0_ffn_bw", "L0_ffn_Wo", "L0_ffn_bo"]
_PATCH = 200


def _dft_table():
    import numpy as np
    n = np.arange(_PATCH)[:, None]
    f = np.arange(_PATCH // 2 + 1)[None, :]
    k = (n * f) % _PATCH
    cos = np.cos(2 * np.pi * k / _PATCH)
    sin = -np.sin(2 * np.pi * k / _PATCH)
    sin[(2 * k) % _PATCH == 0] = 0.0
    both = np.stack([cos, sin], axis=1).reshape(2, _PATCH // 2, 2, _PATCH // 2 + 1)
    return np.ascontiguousarray(both.transpose(1, 0, 2, 3).astype(np.float32))


def kernel(**inputs):
    import numpy as _np
    import concourse.bacc as _bacc
    from concourse import mybir as _mybir
    from concourse.bass_utils import run_bass_kernel_spmd as _run

    nc = _bacc.Bacc("TRN2", target_bir_lowering=False, num_devices=1)
    arrays, args = {}, []
    for name in _INS:
        arrays[f"in_{name}"] = _np.ascontiguousarray(inputs[name])
    arrays["in_dft"] = _dft_table()
    for name, a in arrays.items():
        args.append(nc.dram_tensor(name, a.shape, _mybir.dt.from_np(a.dtype), kind="ExternalInput").ap())
    b, c, n = inputs["x"].shape
    shape = (b, c * (n // _PATCH), inputs["L0_tok_W2"].shape[1])
    args.append(nc.dram_tensor("out_0", shape, _mybir.dt.float32, kind="ExternalOutput").ap())
    audio_tower(nc, *args)
    r = _run(nc, [arrays], core_ids=[0])
    return r.results[0]["out_0"]
```

```python
from contextlib import ExitStack

import concourse.bass as bass
from concourse import mybir

ALU = mybir.AluOpType
ACT = mybir.ActivationFunctionType
F32 = mybir.dt.float32
BF16 = mybir.dt.bfloat16
F16 = mybir.dt.float16
U32 = mybir.dt.uint32
AX = mybir.AxisListType.X

HALF_PI = 1.5707963267948966
TINY = 1e-30
TINY_POWER = 1e-34
EPS = 1e-5
NEWTON = 40
WARM = 14
EARLY = 9
XT_PIECE, SKIP_PIECE = 4, 6
SQRT_PIECE, ATAN_PIECE = 4, 2
SCAN_FROM = 5, 4
WEIGHTS_AT = {(5, 4): 0, (5, 5): 1, (5, 6): 2, (6, 0): 3, (6, 1): 4}
WEIGHT_BANKS = (1, 2, 1, 2, 1)
FIRST_GATES = {1: (0,), 2: (1,), 3: (2,), 4: (3,), 5: (4, 5)}
W_SCALE = 2.0 ** 8
H_SCALE = 2.0 ** 14
G_SCALE = W_SCALE * H_SCALE
W_CLAMP = 60000.0

OUT_AT, NORM_AT, TRANSPOSE_AT, LOGIT_AT, GATES_AT = 2, 4, 5, 6, 7
LAST_ROWS_AT = 2


def audio_tower(nc, x, W1, b1, W2, b2, A, Bm, C, D, log_dt, W_out, b_out,
                Wuz, buz, Wwz, bwz, Wur, bur, Wwr, bwr, Wu, bu, Ww, bw, Wo, bo, dft, out):
    NB, NC, LEN = x.shape
    KP = dft.shape[0]
    PATCH = 2 * KP
    NS = LEN // PATCH
    NF = PATCH // 2 + 1
    T = NC * NS
    NT = T * NB
    HID = W1.shape[1]
    DM = W2.shape[1]
    N = A.shape[0]
    H = Wwz.shape[0]
    KH = H // 128
    CH = 16
    CT = CH * NB
    NCH = T // CH
    MC = -(-HID // 128)
    ML = HID - 128 * (MC - 1)
    NP = 4
    CP = NC // NP
    PT = CP * NS * NB
    HT = PT // 2
    QS = (-(-PT // CT) + 1) // 2, (PT // CT) // 2
    NG = 2 * NP
    GM = QS[0] * CT
    S0 = -(-NS // 2)
    assert CT == 128 and DM == 128 and KH == 2 and CP * NB == 128 and PT % CT == 0 and HT <= 512 and H == 256

    with ExitStack() as ctx:
        def sb(name, shape, dt=F32):
            return ctx.enter_context(nc.sbuf_tensor(name, shape, dt))

        def sem(name):
            return ctx.enter_context(nc.semaphore(name))

        x_sb = sb("x_sb", [128, NP, LEN])
        dft_sb = sb("dft_sb", [KP, 2, 2, NF])
        ident = sb("ident", [128, 128])
        ident_bf = sb("ident_bf", [128, 128], BF16)
        patT = sb("patT", [KP, 2, PT])
        magT = sb("magT", [NF, NT])
        angT = sb("angT", [NF, NT])
        absre = sb("absre", [NF, PT])
        imag = sb("imag", [NF, NP, PT])
        absim = sb("absim", [NF, NP, PT])
        neghalf = sb("neghalf", [NF, NP, PT])
        re2 = sb("re2", [NF, PT])
        im2 = sb("im2", [NF, PT])
        power = sb("power", [NF, PT])
        denom = sb("denom", [NF, PT])
        rdenom = sb("rdenom", [NF, PT])
        expo_ln = sb("expo_ln", [128, QS[0]])
        W1_sb = sb("W1_sb", [NF, 2, HID])
        W2_sb = sb("W2_sb", [128, MC, DM])
        bias_rows = sb("bias_rows", [32, 128])
        spare = sb("spare", [1, 3])
        biasT = sb("biasT", [128, 32])
        bsum = sb("bsum", [128, 3 * KH])
        gbias = sb("gbias", [128, 3 * KH])
        vec_rows = sb("vec_rows", [1, 3, DM])
        ones_row = sb("ones_row", [1, 128])
        ones_sq = sb("ones_sq", [N, N])
        b2_bc = sb("b2_bc", [128, DM])
        bout_bc = sb("bout_bc", [128, DM])
        bo_bc = sb("bo_bc", [128, DM])
        hid = sb("hid", [128, 2, GM])
        h1 = sb("h1", [128, QS[0], DM])
        h1b = sb("h1b", [128, QS[0], DM])
        stats = sb("stats", [128, QS[0], 6])
        mv = sb("mv", [128, QS[0], 2])
        var_eps = sb("var_eps", [128, QS[0]])
        rstd = sb("rstd", [128, QS[0]])
        xln = sb("xln", [128, QS[0], DM])
        xlnT = sb("xlnT", [128, NT])
        hres = sb("hres", [128, NT])
        Wout_sb = sb("Wout_sb", [128, DM])
        WoutT = sb("WoutT", [128, DM])
        WDT = sb("WDT", [128, DM])
        C_sb = sb("C_sb", [DM, N])
        WCT = sb("WCT", [N, DM])
        Dcol = sb("Dcol", [DM, 1])
        A_sb = sb("A_sb", [N, N])
        AT = sb("AT", [N, N])
        B_sb = sb("B_sb", [N, DM])
        dtrow = sb("dtrow", [1, DM])
        dtsum = sb("dtsum", [1, 1])
        dtcol = sb("dtcol", [128, 1])
        negdt = sb("negdt", [128, 1])
        Mt = sb("Mt", [N, 2, N])
        sq = sb("sq", [N, N])
        sqsum = sb("sqsum", [N, 1])
        scale0 = sb("scale0", [N, 1])
        negMT = sb("negMT", [128, N])
        eye = sb("eye", [128, N])
        eye2 = sb("eye2", [128, N])
        XY = sb("XY", [128, 2, N])
        Dn = sb("Dn", [128, N])
        AbarT = sb("AbarT", [128, N])
        BbarT = sb("BbarT", [DM, N])
        states = sb("states", [128, CT])
        wnat = sb("wnat", [128, 3, KH, H])
        wunat = sb("wunat", [128, 3, KH, DM])
        wonat = sb("wonat", [DM, H])
        wT = sb("wT", [128, 3, KH * H])
        wres = sb("wres", [128, 3, KH * H])
        w_first = sb("w_first", [128, 3, KH, H], F16)
        w_rest = sb("w_rest", [128, 2, 3, KH, H], BF16)
        WuT = sb("WuT", [128, 3 * KH, 128])
        WoT = sb("WoT", [128, KH, DM])
        h2 = sb("h2", [128, DM])
        stats2 = sb("stats2", [128, 6])
        mv2 = sb("mv2", [128, 2])
        vare2 = sb("vare2", [128, 1])
        rstd2 = sb("rstd2", [128, 1])
        x2 = sb("x2", [128, DM])
        x2T = sb("x2T", [128, CT])
        gin = sb("gin", [128, CH, 3, KH * NB])
        gparts = sb("gparts", [128, 3, CH, 3, KH * NB], BF16)
        gres = sb("gres", [128, CH // 2, KH * NB])
        SW = KH * NB
        tanh_r = sb("tanh_r", [128, SW])
        tanh_z = sb("tanh_z", [128, SW])
        zgate = sb("zgate", [128, SW])
        coef = sb("coef", [128, SW, 2])
        addend = sb("addend", [128, SW, 2])
        h_hi = sb("h_hi", [128, SW, 2], F16)
        h_lo = sb("h_lo", [128, SW], F16)
        hseq = sb("hseq", [128, CH, SW, 2])
        rh = sb("rh", [128, SW])
        rh_hi = sb("rh_hi", [128, SW], F16)
        rh_lo = sb("rh_lo", [128, SW], F16)
        hchunk = sb("hchunk", [128, KH, CH, NB])
        logit = sb("logit", [128, DM])
        tanh_o = sb("tanh_o", [128, DM])
        sig_o = sb("sig_o", [128, DM])
        res = sb("res", [128, DM])

        ps = ctx.enter_context(nc.psum_tensor("ps", [128, 8, 512], F32))

        def bank(i, p=128, w=512):
            return ps[0:p, i, 0:w]

        def ps_patT(k, g, h):
            return bank(k + (4 if (g, h) == (0, 1) else 0), KP)

        def ps_re(g, h):
            return bank(6 if (g, h) == (0, 1) else 2, NF, HT)

        def ps_im(g, h):
            return bank(7 if (g, h) == (0, 1) else 3, NF, HT)

        ps_hid = [bank(4), bank(5)]
        ps_out, ps_row = bank(6), bank(7)
        ps_gate = [bank(4 + g, 128, SW) for g in range(3)]
        ps_s = [bank(0, N, CT // 2), bank(3, N, CT // 2)]
        ps_p = bank(2, 128, CT)
        ps_x = [bank(1, 128, CT), ps_p]
        ps_o = bank(7, 128, DM)

        x_in = [sem(f"x_in{g}") for g in range(NP)]
        dft_in = sem("dft_in")
        tok_in = sem("tok_in")
        rows_in = sem("rows_in")
        dt_in = sem("dt_in")
        a_in = sem("a_in")
        ssm_in = sem("ssm_in")
        gru_in = sem("gru_in")
        consts = sem("consts")
        pool_passed = sem("pool_passed")
        dve_passed = sem("dve_passed")
        bf_ident = sem("bf_ident")
        patT_psum = sem("patT_psum")
        patT0_copied = sem("patT0_copied")
        patT1_copied = sem("patT1_copied")
        spec_psum = sem("spec_psum")
        absre_done = sem("absre_done")
        rden_done = sem("rden_done")
        fold_done = sem("fold_done")
        re_read = sem("re_read")
        im_read = sem("im_read")
        re2_im2 = sem("re2_im2")
        absim_done = sem("absim_done")
        power_done = sem("power_done")
        mag_done = sem("mag_done")
        den_done = sem("den_done")
        tang_done = sem("tang_done")
        atan_done = sem("atan_done")
        sign_done = sem("sign_done")
        ang_done = sem("ang_done")
        su_act = sem("su_act")
        su_dve = sem("su_dve")
        su_pool = sem("su_pool")
        su_pe = sem("su_pe")
        bias_psum = sem("bias_psum")
        sq_psum = sem("sq_psum")
        b_psum = sem("b_psum")
        c_w_psum = sem("c_w_psum")
        wct_done = sem("wct_done")
        wT_done = sem("wT_done")
        wp_done = [sem(f"wp_done{g}") for g in range(3)]
        hid_psum = sem("hid_psum")
        gelu_done = sem("gelu_done")
        out_psum = sem("out_psum")
        out_read = sem("out_read")
        st_done = sem("st_done")
        mv_done = sem("mv_done")
        ve_done = sem("ve_done")
        rstd_done = sem("rstd_done")
        xln_done = sem("xln_done")
        xT_psum = sem("xT_psum")
        xT_copied = sem("xT_copied")
        h1b_done = sem("h1b_done")
        y0_psum = sem("y0_psum")
        y0_read = sem("y0_read")
        nt_psum = sem("nt_psum")
        dn_done = sem("dn_done")
        nx_psum = sem("nx_psum")
        xy_done = sem("xy_done")
        bar_done = sem("bar_done")
        s_psum = sem("s_psum")
        s_done = sem("s_done")
        p_psum = sem("p_psum")
        h2_done = sem("h2_done")
        st2_done = sem("st2_done")
        mv2_done = sem("mv2_done")
        h2_stored = sem("h2_stored")
        ve2_done = sem("ve2_done")
        rstd2_done = sem("rstd2_done")
        x2_done = sem("x2_done")
        x2T_psum = sem("x2T_psum")
        x2T_done = sem("x2T_done")
        gx_psum = sem("gx_psum")
        gin_done = sem("gin_done")
        gp_chain = sem("gp_chain")
        h_hi_done = sem("h_hi_done")
        h_full = sem("h_full")
        h_lo_done = sem("h_lo_done")
        r_psum = sem("r_psum")
        z_psum = sem("z_psum")
        c_psum = sem("c_psum")
        r_done = sem("r_done")
        z_done = sem("z_done")
        c_done = sem("c_done")
        rh_hi_done = sem("rh_hi_done")
        rh_full = sem("rh_full")
        rh_lo_done = sem("rh_lo_done")
        zg_done = sem("zg_done")
        zh_done = sem("zh_done")
        hchunk_done = sem("hchunk_done")
        o_psum = sem("o_psum")
        logit_done = sem("logit_done")
        tanho_done = sem("tanho_done")
        sigo_done = sem("sigo_done")
        res_done = sem("res_done")
        out_dma = sem("out_dma")

        def tile(t, g):
            return t[:, PT * g:PT * (g + 1)]

        def half_of(t, h):
            return t[:, h * HT:(h + 1) * HT]

        def patches(h):
            s0, s1 = (0, S0) if h == 0 else (S0, NS)
            return s0, s1, slice(128 * s0, 128 * s1)

        def group(n):
            return PT * (n // 2) + (n % 2) * GM, QS[n % 2]

        def msize(m):
            return 128 if m < MC - 1 else ML

        def gate_cols(m):
            return slice(m * NB, (m + 1) * NB)

        HALVES = 2 * NEWTON

        def blocked(n, m, slot):
            if slot == 1 and (n % 2 or n >= NG - 2 or m not in (1, 2, 3)):
                return True
            if n in (2, 4) and slot == 2 and m in (XT_PIECE, SKIP_PIECE):
                return True
            if n in (0, 2, 4) and (m, slot) == (SQRT_PIECE + 2, 0):
                return True
            return n in (1, 3, 5) and (m, slot) in ((ATAN_PIECE + 1, 2), (ATAN_PIECE + 2, 0))

        SLOTS, taken = {}, EARLY
        SCANS, scanned = {}, 0
        for n in range(NG):
            for m in range(MC):
                for slot in range(3):
                    if blocked(n, m, slot):
                        continue
                    if taken < HALVES:
                        SLOTS[n, m, slot] = taken
                        taken += 1
                    if (n, m) >= SCAN_FROM and scanned < 2 * CH:
                        SCANS[n, m, slot] = scanned
                        scanned += 1
        assert taken == HALVES and scanned == 2 * CH and (SCAN_FROM[0], SCAN_FROM[1] - 1, 2) not in SLOTS

        def newton_bank(i):
            at = [key[0] for key, j in SLOTS.items() if j == i]
            b = 2 if at and (at[0] % 2) else 7
            return bank(b, N, N), bank(b, N, 2 * N)

        OUT_T = out.rearrange("b t d -> t b d")

        def split_weights(eng, ops, g):
            src, rest, done = wT[:, g, :], wres[:, g, :], wp_done[g]
            part = [w.rearrange("p k h -> p (k h)") for w in (w_first[:, g], w_rest[:, 0, g], w_rest[:, 1, g])]
            eng.wait_ge(wT_done, g + 1)
            ops.tensor_scalar(part[0], src, W_CLAMP, -W_CLAMP, ALU.min, ALU.max).then_inc(done, 1)
            eng.wait_ge(done, 1)
            ops.tensor_tensor(rest, src, part[0], ALU.subtract).then_inc(done, 1)
            eng.wait_ge(done, 2)
            ops.tensor_copy(part[1], rest).then_inc(done, 1)
            eng.wait_ge(done, 3)
            ops.tensor_tensor(part[2], rest, part[1], ALU.subtract).then_inc(done, 1)

        def scan(v, dst):
            return v.tensor_tensor_scan(out=dst, data0=coef[:].rearrange("p s i -> p (s i)"),
                                        data1=addend[:].rearrange("p s i -> p (s i)"), initial=0.0,
                                        op0=ALU.mult, op1=ALU.add)

        block = ctx.enter_context(nc.Block())

        @block.sync
        def _(sp):
            def load(g):
                sp.dma_start(x_sb[:, g, :], x[:, CP * g:CP * (g + 1), :]).then_inc(x_in[g], 16)

            load(0)
            sp.dma_start(dft_sb[:], dft).then_inc(dft_in, 16)
            load(1)
            sp.dma_start(B_sb[:], Bm).then_inc(ssm_in, 16)
            sp.dma_start(C_sb[:], C).then_inc(ssm_in, 16)
            sp.dma_start(Dcol[:], D.rearrange("(d a) -> d a", a=1)).then_inc(ssm_in, 16)
            sp.dma_start(Wout_sb[:], W_out).then_inc(ssm_in, 16)
            for i, v in enumerate((b2, b_out, bo)):
                sp.dma_start(vec_rows[:, i, :], v.rearrange("(a d) -> a d", a=1)).then_inc(ssm_in, 16)
            for g in range(2, NP):
                load(g)
            sp.dma_start(W1_sb[:], W1.rearrange("(k p) h -> p k h", p=NF)).then_inc(tok_in, 16)
            sp.dma_start(W2_sb[:, 0:MC - 1, :],
                         W2[0:128 * (MC - 1), :].rearrange("(m p) d -> p m d", p=128)).then_inc(tok_in, 16)
            sp.dma_start(W2_sb[0:ML, MC - 1, :], W2[128 * (MC - 1):HID, :]).then_inc(tok_in, 16)
            for g, (w, u) in enumerate(((Wwr, Wur), (Wwz, Wuz), (Ww, Wu))):
                sp.dma_start(wnat[:, g, :, :], w.rearrange("(m p) k -> p m k", p=128)).then_inc(gru_in, 16)
                sp.dma_start(wunat[:, g, :, :], u.rearrange("(m p) k -> p m k", p=128)).then_inc(gru_in, 16)
            sp.dma_start(wonat[:], Wo).then_inc(gru_in, 16)

            def store(c):
                sp.wait_ge(res_done, c + 1)
                sp.dma_start(OUT_T[bass.ds(c * CH, CH)], res[:]).then_inc(out_dma, 16)

            with sp.Fori(0, NCH) as c:
                store(c)
            sp.wait_ge(out_dma, 16 * NCH)

        @block.gpsimd
        def _(pool):
            pool.memset(ident[:], 0.0).then_inc(su_pool, 1)
            pool.memset(bias_rows[:], 0.0).then_inc(su_pool, 1)
            pool.wait_ge(su_pool, 2)
            pool.affine_select(out=ident[:], in_=ident[:], compare_op=ALU.not_equal, fill=1.0, base=0,
                               pattern=[[-1, 128]], channel_multiplier=1).then_inc(consts, 1)
            pool.memset(ones_row[:], 1.0).then_inc(consts, 1)
            pool.memset(ones_sq[:], 1.0).then_inc(consts, 1)
            pool.memset(expo_ln[:], -0.5).then_inc(consts, 1)
            for z in (XY[:].rearrange("p a n -> p (a n)"), Dn[:], negMT[:], AbarT[:], states[:]):
                pool.memset(z, 0.0).then_inc(consts, 1)
            pool.memset(coef[:].rearrange("p a n -> p (a n)"), 0.0).then_inc(consts, 1)
            pool.memset(addend[:].rearrange("p a n -> p (a n)"), 0.0).then_inc(consts, 1)
            pool.memset(hseq[:].rearrange("p a b n -> p (a b n)"), 0.0).then_inc(consts, 1)
            pool.memset(h_hi[:].rearrange("p a n -> p (a n)"), 0.0).then_inc(consts, 1)
            pool.memset(h_lo[:], 0.0).then_inc(consts, 1)
            pool.wait_ge(consts, 1)
            pool.tensor_copy(ident_bf[:], ident[:]).then_inc(bf_ident, 1)
            pool.tensor_copy(eye[:], ident[:, 0:N]).then_inc(bf_ident, 1)
            pool.tensor_scalar(eye2[:], ident[:, 0:N], 2.0, None, ALU.mult).then_inc(bf_ident, 1)

            pool.dma_start(bias_rows[0:MC - 1, :],
                           b1[0:128 * (MC - 1)].rearrange("(m p) -> m p", p=128)).then_inc(rows_in, 16)
            pool.dma_start(bias_rows[MC - 1:MC, 0:ML],
                           b1[128 * (MC - 1):HID].rearrange("(m p) -> m p", m=1)).then_inc(rows_in, 16)
            for i, v in enumerate((bur, buz, bu, bwr, bwz, bw)):
                r = MC + KH * i
                pool.dma_start(bias_rows[r:r + KH, :],
                               v.rearrange("(m p) -> m p", p=128)).then_inc(rows_in, 16)

            def tangent(g):
                for h in range(2):
                    v = half_of(absim[:, g, :], h)
                    pool.wait_ge(rden_done, 2 * g + h + 1)
                    pool.wait_ge(absim_done, 2 * g + h + 1)
                    pool.tensor_tensor(v, v, half_of(rdenom, h), ALU.mult).then_inc(tang_done, 1)

            def fold(g):
                for h in range(2):
                    pool.wait_ge(atan_done, 2 * g + h + 1)
                    pool.tensor_tensor(half_of(neghalf[:, g, :], h), half_of(absim[:, g, :], h),
                                       half_of(neghalf[:, g, :], h), ALU.subtract).then_inc(fold_done, 1)

            def tok_head(n):
                nq = group(n)[1]
                pool.wait_ge(mv_done, n + 1)
                pool.tensor_scalar(var_eps[:, 0:nq], mv[:, 0:nq, 1], EPS, None, ALU.add).then_inc(ve_done, 1)
                pool.wait_ge(ve_done, n + 1)
                pool.tensor_tensor(rstd[:, 0:nq], var_eps[:, 0:nq], expo_ln[:, 0:nq], ALU.pow).then_inc(rstd_done, 1)
                if n:
                    pool.wait_ge(y0_read, n)
                pool.wait_ge(out_read, n + 1)
                for q in range(nq):
                    last = pool.tensor_tensor(h1b[:, q, :], h1[:, q, :], bout_bc[:], ALU.add)
                last.then_inc(h1b_done, 1)

            def split(c, half, g):
                s0 = half * (CH // 2)
                base = 24 * c + 12 * half + 4 * g
                src = gin[:, s0:s0 + CH // 2, g, :]
                part = [gparts[:, i, s0:s0 + CH // 2, g, :] for i in range(3)]
                pool.wait_ge(gin_done, 6 * c + 2 * g + 2)
                pool.sem_inc(pool_passed, 1)
                pool.tensor_copy(part[0], src).then_inc(gp_chain, 1)
                pool.wait_ge(gp_chain, base + 1)
                pool.tensor_tensor(gres[:], src, part[0], ALU.subtract).then_inc(gp_chain, 1)
                pool.wait_ge(gp_chain, base + 2)
                pool.sem_inc(pool_passed, 1)
                pool.tensor_copy(part[1], gres[:]).then_inc(gp_chain, 1)
                pool.wait_ge(gp_chain, base + 3)
                pool.tensor_tensor(part[2], gres[:], part[1], ALU.subtract).then_inc(gp_chain, 1)

            def post(c):
                pool.wait_ge(mv2_done, c + 1)
                pool.sem_inc(pool_passed, 1)
                pool.tensor_scalar(vare2[:], mv2[:, 1:2], EPS, None, ALU.add).then_inc(ve2_done, 1)
                pool.wait_ge(ve2_done, c + 1)
                pool.tensor_tensor(rstd2[:], vare2[:], expo_ln[:, 0:1], ALU.pow).then_inc(rstd2_done, 1)
                pool.tensor_copy(hres[:, bass.ds(c * DM, DM)], h2[:]).then_inc(h2_stored, 1)

            def copy_states(c, half):
                s0 = half * (CH // 2)
                pool.wait_ge(h_full, CH * c + s0 + CH // 2)
                pool.sem_inc(pool_passed, 1)
                pool.tensor_copy(hchunk[:, :, s0:s0 + CH // 2].rearrange("p k t b -> p t k b"),
                                 hseq[:, s0:s0 + CH // 2, :, 1].rearrange("p t (k b) -> p t k b", k=KH)
                                 ).then_inc(hchunk_done, 1)

            def result(c, first):
                pool.wait_ge(tanho_done, c + 1)
                pool.sem_inc(pool_passed, 1)
                pool.tensor_scalar(sig_o[:], tanh_o[:], 0.5, 0.5, ALU.mult, ALU.add).then_inc(sigo_done, 1)
                if not first:
                    pool.wait_ge(out_dma, 16 * c)
                pool.wait_ge(sigo_done, c + 1)
                pool.sem_inc(pool_passed, 1)
                pool.tensor_tensor(res[:], sig_o[:], hres[:, bass.ds(c * DM, DM)],
                                   ALU.add).then_inc(res_done, 1)

            def body(c, first, last, first_store=False):
                if not first:
                    copy_states(c - 1, 1)
                    pool.wait_ge(c_psum, CH * c)
                split(c, 1, 0)
                split(c, 1, 1)
                if not last:
                    post(c + 1)
                split(c, 1, 2)
                if not first:
                    result(c - 1, first_store)
                    pool.wait_ge(o_psum, c)
                copy_states(c, 0)
                if not last:
                    pool.wait_ge(c_psum, CH * c + CH // 2)
                    for g in range(3):
                        split(c + 1, 0, g)

            tangent(0)
            fold(0)
            pool.wait_ge(su_act, 5)
            for n in range(1, NG):
                g = (n + 1) // 2
                if n % 2 and g < NP:
                    tangent(g)
                if n == NG - 1:
                    post(0)
                tok_head(n - 1)
                if n % 2 and g < NP:
                    fold(g)
                if n == NG - 3:
                    split_weights(pool, pool, 0)

            for g in range(3):
                split(0, 0, g)
            tok_head(NG - 1)
            body(0, True, False)
            body(1, False, False, True)
            with pool.Fori(2, NCH - 1) as c:
                body(c, False, False)
            body(NCH - 1, False, True)
            copy_states(NCH - 1, 1)
            result(NCH - 1, False)

        @block.scalar
        def _(act):
            a = nc.scalar
            act.dma_start(dtrow[:], log_dt.rearrange("(a d) -> a d", a=1)).then_inc(dt_in, 16)
            act.dma_start(A_sb[:], A).then_inc(a_in, 16)

            def copy_patches(g, h):
                cols = patches(h)[2]
                act.wait_ge(patT_psum, 2 * g + h + 1)
                if g and h == 0:
                    act.wait_ge(spec_psum, 2 * g)
                a.activation(patT[:, 0, cols], ps_patT(0, g, h)[:, 0:cols.stop - cols.start],
                             ACT.Copy).then_inc(patT0_copied, 1)

            def abs_re(g, h):
                act.wait_ge(spec_psum, 2 * g + h + 1)
                if g and h == 0:
                    act.wait_ge(ang_done, g)
                a.activation(absre[:, h * HT:(h + 1) * HT], ps_re(g, h), ACT.Abs).then_inc(absre_done, 1)

            def square_re(g, h):
                act.wait_ge(absre_done, 2 * g + h + 1)
                a.activation(half_of(re2, h), half_of(absre, h), ACT.Square).then_inc(re2_im2, 1)

            def square_im(g, h):
                act.wait_ge(im_read, 2 * g + h + 1)
                a.activation(half_of(im2, h), half_of(imag[:, g, :], h), ACT.Square).then_inc(re2_im2, 1)

            def abs_im(g, h):
                a.activation(half_of(absim[:, g, :], h), half_of(imag[:, g, :], h), ACT.Abs).then_inc(absim_done, 1)

            def magnitude(g):
                for h in range(2):
                    act.wait_ge(power_done, 2 * g + h + 1)
                    a.activation(half_of(tile(magT, g), h), half_of(power, h), ACT.Sqrt).then_inc(mag_done, 1)

            def arctangent(g):
                for h in range(2):
                    v = half_of(absim[:, g, :], h)
                    act.wait_ge(tang_done, 2 * g + h + 1)
                    a.activation(v, v, ACT.Arctan).then_inc(atan_done, 1)

            def load_table(i, f):
                a.activation(spare[:, i:i + 1], ones_row[:, 0:1], f)

            def newton(i):
                ps_nt, ps_nx = newton_bank(i)
                if i % 2 == 0:
                    act.wait_ge(nt_psum, i // 2 + 1)
                    a.activation(Dn[0:N, :], ps_nt, ACT.Copy).then_inc(dn_done, 1)
                else:
                    act.wait_ge(nx_psum, i // 2 + 1)
                    a.activation(XY[0:N].rearrange("p a n -> p (a n)"), ps_nx, ACT.Copy).then_inc(xy_done, 1)

            for h in range(2):
                copy_patches(0, h)
            act.wait_ge(dt_in, 16)
            a.activation(dtrow[:], dtrow[:], ACT.Exp).then_inc(su_act, 1)
            act.wait_ge(consts, 14)
            load_table(0, ACT.Sqrt)
            act.wait_ge(su_pe, 1)
            a.activation(dtcol[:], bank(5)[:, 0:1], ACT.Copy, scale=1.0 / DM).then_inc(su_act, 1)
            for h in range(2):
                abs_re(0, h)
                square_re(0, h)
                square_im(0, h)
                abs_im(0, h)
            newton(0)
            magnitude(0)
            newton(1)
            load_table(1, ACT.Arctan)
            newton(2)
            act.wait_ge(su_pe, 3)
            a.activation(WoutT[:], bank(5)[:, 0:128], ACT.Copy).then_inc(su_act, 1)
            a.activation(b2_bc[:], bank(2)[:, 0:DM], ACT.Copy)
            a.activation(bout_bc[:], bank(2)[:, DM:2 * DM], ACT.Copy).then_inc(su_act, 1)
            a.activation(bo_bc[:], bank(2)[:, 2 * DM:3 * DM], ACT.Copy).then_inc(su_act, 1)
            for i in range(3, EARLY):
                newton(i)
            copy_patches(1, 0)
            arctangent(0)
            load_table(2, ACT.Gelu)
            act.wait_ge(bias_psum, 1)
            a.activation(biasT[:], bank(4)[:, 0:32], ACT.Copy).then_inc(su_act, 1)
            copy_patches(1, 1)

            def ssm_tanh(c, k):
                act.wait_ge(s_psum, CH * c + k + 1)
                k1 = k % (CH // 2)
                a.activation(states[0:N, k * NB:(k + 1) * NB], ps_s[k // (CH // 2)][:, k1 * NB:(k1 + 1) * NB],
                             ACT.Tanh).then_inc(s_done, 1)

            def copy_weights(i):
                act.wait_ge(su_pe, 4 + i)
                if i < 3:
                    a.activation(wT[:, i, :], bank(WEIGHT_BANKS[i]), ACT.Copy,
                                 scale=W_SCALE * (0.5 if i == 2 else 1.0)).then_inc(wT_done, 1)
                elif i == 3:
                    a.activation(WuT[:, 0:4, :].rearrange("p a d -> p (a d)"), bank(WEIGHT_BANKS[3]), ACT.Copy,
                                 scale=G_SCALE).then_inc(wT_done, 1)
                else:
                    b = WEIGHT_BANKS[4]
                    a.activation(WuT[:, 4:6, :].rearrange("p a d -> p (a d)"), ps[:, b, 0:256], ACT.Copy,
                                 scale=G_SCALE)
                    a.activation(WoT[:].rearrange("p a d -> p (a d)"), ps[:, b, 256:512], ACT.Copy,
                                 scale=1.0 / H_SCALE).then_inc(wT_done, 1)

            def copy_xT(n):
                t0, nq = group(n)
                act.wait_ge(xT_psum, n + 1)
                a.activation(xlnT[:, t0:t0 + nq * CT], ps_row[:, 0:nq * CT], ACT.Copy).then_inc(xT_copied, 1)

            def copy_x2T(c):
                act.wait_ge(x2T_psum, c + 1)
                a.activation(x2T[:], ps_p, ACT.Copy).then_inc(x2T_done, 1)

            def copy_gin(c, i, first):
                g, m = i // KH, i % KH
                act.wait_ge(gx_psum, 3 * KH * c + i + 1)
                if not first and i == 0:
                    act.wait_ge(gp_chain, 24 * c)
                a.activation(gin[:, :, g, gate_cols(m)],
                             ps_x[i % 2].rearrange("p (t b) -> p t b", b=NB),
                             ACT.Identity, bias=gbias[:, i:i + 1]).then_inc(gin_done, 1)

            def serial(n, m, slot):
                if (n, m, slot) in SLOTS:
                    newton(SLOTS[n, m, slot])
                if (n, m, slot) in SCANS:
                    k = SCANS[n, m, slot]
                    ssm_tanh(k // CH, k % CH)

            for n in range(NG):
                nt = group(n)[1] * CT
                g = n // 2 + 1
                for m in range(MC):
                    p = MC * n + m
                    k = msize(m)
                    serial(n, m, 0)
                    act.wait_ge(hid_psum, p + 1)
                    a.activation(hid[0:k, p % 2, 0:nt], ps_hid[p % 2][0:k, 0:nt], ACT.Gelu,
                                 bias=biasT[0:k, m:m + 1]).then_inc(gelu_done, 1)
                    if n == NG - 1 and m == 0:
                        copy_x2T(0)
                    if n == NG - 1 and m - 1 in FIRST_GATES:
                        for i in FIRST_GATES[m - 1]:
                            copy_gin(0, i, True)
                    serial(n, m, 1)
                    serial(n, m, 2)
                    if n and m == XT_PIECE:
                        copy_xT(n - 1)
                    if n % 2 == 0 and g < NP:
                        if m == 1:
                            abs_re(g, 0)
                        if m == 2:
                            square_re(g, 0)
                            square_im(g, 0)
                            abs_im(g, 0)
                        if m == 3:
                            abs_re(g, 1)
                            square_re(g, 1)
                            square_im(g, 1)
                        if m == SQRT_PIECE + 1:
                            abs_im(g, 1)
                        if m == SQRT_PIECE:
                            magnitude(g)
                    if n % 2 == 1 and g < NP and m == ATAN_PIECE:
                        arctangent(g)
                    if n % 2 == 1 and g + 1 < NP and m in (4, 6):
                        copy_patches(g + 1, m // 2 - 2)
                    if (n, m) in WEIGHTS_AT:
                        copy_weights(WEIGHTS_AT[n, m])
                    if (n, m + 1) == SCAN_FROM:
                        act.wait_ge(c_w_psum, 1)
                        a.activation(WCT[:], bank(3)[0:N, 0:DM], ACT.Copy).then_inc(wct_done, 1)

            ssm_tanh(2, 0)

            def body(c, out_before, post_next, scan_2, scan_3):
                for j in range(CH):
                    t = CH * c + j
                    act.wait_ge(r_psum, t + 1)
                    a.activation(tanh_r[:], ps_gate[0], ACT.Tanh, scale=0.5 / G_SCALE).then_inc(r_done, 1)
                    act.wait_ge(z_psum, t + 1)
                    a.activation(tanh_z[:], ps_gate[1], ACT.Tanh, scale=0.5 / G_SCALE).then_inc(z_done, 1)
                    if scan_2 and j < CH - 1:
                        ssm_tanh(c + 2, j + 1)
                    if scan_3 and j == CH - 1:
                        ssm_tanh(c + 3, 0)
                    act.wait_ge(c_psum, t + 1)
                    a.activation(addend[:, :, 0], ps_gate[2], ACT.Tanh, scale=1.0 / G_SCALE).then_inc(c_done, 1)
                    if not out_before and j == LAST_ROWS_AT + 1:
                        copy_xT(NG - 1)
                    if post_next and j == TRANSPOSE_AT + 1:
                        copy_x2T(c + 1)
                    if post_next and 0 <= j - GATES_AT - 1 < 3 * KH:
                        copy_gin(c + 1, j - GATES_AT - 1, False)
                    if out_before and j == LOGIT_AT + 1:
                        act.wait_ge(logit_done, c)
                        a.activation(tanh_o[:], logit[:], ACT.Tanh, scale=0.5).then_inc(tanho_done, 1)

            body(0, False, True, True, True)
            with act.Fori(1, NCH - 3) as c:
                body(c, True, True, True, True)
            body(NCH - 3, True, True, True, False)
            body(NCH - 2, True, True, False, False)
            body(NCH - 1, True, False, False, False)
            act.wait_ge(logit_done, NCH)
            a.activation(tanh_o[:], logit[:], ACT.Tanh, scale=0.5).then_inc(tanho_done, 1)

        @block.vector
        def _(dve):
            v = nc.vector
            def copy_patches(g, h):
                cols = patches(h)[2]
                dve.wait_ge(patT_psum, 2 * g + h + 1)
                if g and h == 0:
                    dve.wait_ge(spec_psum, 2 * g)
                v.tensor_scalar(patT[:, 1, cols], ps_patT(1, g, h)[:, 0:cols.stop - cols.start], 0.0, None,
                                ALU.add).then_inc(patT1_copied, 1)

            def read_spectra(g, h):
                cols = slice(h * HT, (h + 1) * HT)
                dve.wait_ge(spec_psum, 2 * g + h + 1)
                v.tensor_scalar(imag[:, g, cols], ps_im(g, h), 0.0, None, ALU.add).then_inc(im_read, 1)
                dve.wait_ge(absre_done, 2 * g + h + 1)
                v.tensor_scalar(neghalf[:, g, cols], ps_re(g, h), 0.0, HALF_PI, ALU.is_lt,
                                ALU.mult).then_inc(re_read, 1)

            def add_power(g, h):
                dve.wait_ge(re2_im2, 4 * g + 2 * h + 2)
                v.scalar_tensor_tensor(out=half_of(power, h), in0=half_of(re2, h), scalar=TINY_POWER,
                                       in1=half_of(im2, h), op0=ALU.max, op1=ALU.add).then_inc(power_done, 1)

            def denominator(g):
                for h in range(2):
                    dve.wait_ge(mag_done, 2 * g + h + 1)
                    v.scalar_tensor_tensor(out=half_of(denom, h), in0=half_of(absre, h), scalar=TINY,
                                           in1=half_of(tile(magT, g), h), op0=ALU.max,
                                           op1=ALU.add).then_inc(den_done, 1)

            def invert(g, h):
                dve.wait_ge(den_done, 2 * g + h + 1)
                v.reciprocal(half_of(rdenom, h), half_of(denom, h)).then_inc(rden_done, 1)

            def sign(g):
                dve.wait_ge(absim_done, 2 * g + 2)
                v.tensor_scalar(imag[:, g, :].bitcast(U32), imag[:, g, :].bitcast(U32), 0x80000000, None,
                                ALU.bitwise_and).then_inc(sign_done, 1)

            def angle(g):
                dve.wait_ge(sign_done, g + 1)
                for h in range(2):
                    dve.wait_ge(fold_done, 2 * g + h + 1)
                    last = v.scalar_tensor_tensor(
                        out=half_of(tile(angT, g), h).bitcast(U32), in0=half_of(neghalf[:, g, :], h).bitcast(U32),
                        scalar=0x7fffffff, in1=half_of(imag[:, g, :], h).bitcast(U32),
                        op0=ALU.bitwise_and, op1=ALU.bitwise_or)
                last.then_inc(ang_done, 1)

            for h in range(2):
                copy_patches(0, h)
            dve.wait_ge(su_act, 1)
            v.tensor_scalar(dtrow[:], dtrow[:], 1e-4, 1.0, ALU.max, ALU.min).then_inc(su_dve, 1)
            dve.wait_ge(su_dve, 1)
            v.reduce_sum(dtsum[:], dtrow[:], AX).then_inc(su_dve, 1)
            dve.wait_ge(a_in, 16)
            v.transpose(AT[:], A_sb[:]).then_inc(su_dve, 1)

            read_spectra(0, 0)
            dve.wait_ge(su_act, 2)
            v.tensor_scalar(negdt[:], dtcol[:], -0.5, None, ALU.mult).then_inc(su_dve, 1)
            dve.wait_ge(su_dve, 4)
            dve.wait_ge(bf_ident, 3)
            dve.wait_ge(consts, 14)
            for i, src in enumerate((AT, A_sb)):
                v.scalar_tensor_tensor(out=Mt[:, i, :], in0=src[:], scalar=negdt[0:N, :], in1=eye[0:N, :],
                                       op0=ALU.mult, op1=ALU.add).then_inc(su_dve, 1)
            dve.wait_ge(su_dve, 6)
            v.tensor_tensor(sq[:], Mt[:, 0, :], Mt[:, 0, :], ALU.mult).then_inc(su_dve, 1)
            v.tensor_scalar(negMT[0:N, :], Mt[:, 0, :], -1.0, None, ALU.mult).then_inc(su_dve, 1)
            dve.wait_ge(su_dve, 8)
            v.reduce_sum(sqsum[:], sq[:], AX).then_inc(su_dve, 1)
            add_power(0, 0)
            dve.wait_ge(sq_psum, 1)
            v.reciprocal(scale0[:], bank(5)[0:N, 0:1]).then_inc(su_dve, 1)
            dve.wait_ge(su_dve, 10)
            v.tensor_scalar(XY[0:N].rearrange("p a n -> p (a n)"), Mt[:].rearrange("p a n -> p (a n)"),
                            scale0[:, 0:1], None, ALU.mult).then_inc(su_dve, 1)
            read_spectra(0, 1)
            add_power(0, 1)
            denominator(0)
            invert(0, 0)
            invert(0, 1)
            sign(0)
            dve.wait_ge(su_act, 3)
            v.tensor_scalar(WDT[:], WoutT[:], Dcol[:, 0:1], None, ALU.mult).then_inc(su_dve, 1)
            dve.wait_ge(tok_in, 48)
            v.tensor_scalar(W1_sb[:, 1, :], W1_sb[:, 1, :], 2.0, None, ALU.mult).then_inc(su_dve, 1)
            copy_patches(1, 0)
            angle(0)
            copy_patches(1, 1)
            dve.wait_ge(su_act, 6)
            v.tensor_tensor(bsum[:], biasT[:, MC:MC + 3 * KH], biasT[:, MC + 3 * KH:MC + 6 * KH],
                            ALU.add).then_inc(su_dve, 1)
            dve.wait_ge(su_dve, 14)
            v.tensor_scalar(gbias[:], bsum[:], G_SCALE, None, ALU.mult).then_inc(su_dve, 1)

            def residual(n):
                t0, nq = group(n)
                dve.wait_ge(y0_psum, n + 1)
                dve.wait_ge(h1b_done, n + 1)
                v.tensor_tensor(hres[:, t0:t0 + nq * DM], ps_row[:, 0:nq * DM],
                                h1b[:, 0:nq, :].rearrange("p q d -> p (q d)"), ALU.add).then_inc(y0_read, 1)

            def add_rows(n):
                nq = group(n)[1]
                dve.wait_ge(out_psum, n + 1)
                dve.wait_ge(su_act, 5)
                if n:
                    dve.wait_ge(h1b_done, n)
                for q in range(nq):
                    last = v.tensor_tensor(h1[:, q, :], ps_out[:, q * DM:(q + 1) * DM], b2_bc[:], ALU.add)
                last.then_inc(out_read, 1)

            def moments(n):
                nq = group(n)[1]
                dve.wait_ge(out_read, n + 1)
                for q in range(nq):
                    last = v.bn_stats(stats[:, q, :], h1[:, q, :])
                last.then_inc(st_done, 1)
                dve.wait_ge(st_done, n + 1)
                for q in range(nq):
                    last = v.bn_aggr(mv[:, q, :], stats[:, q, :])
                last.then_inc(mv_done, 1)

            def norm(n):
                dve.wait_ge(rstd_done, n + 1)
                for q in range(group(n)[1]):
                    last = v.tensor_scalar(xln[:, q, :], h1[:, q, :], mv[:, q, 0:1], rstd[:, q:q + 1],
                                           ALU.subtract, ALU.mult)
                last.then_inc(xln_done, 1)

            def post_h2(c, first):
                dve.wait_ge(p_psum, c + 1)
                if not first:
                    dve.wait_ge(h2_stored, c)
                v.tensor_tensor(h2[:], ps_p, hres[:, bass.ds(c * DM, DM)], ALU.add).then_inc(h2_done, 1)

            def post_stats(c):
                dve.wait_ge(h2_done, c + 1)
                v.bn_stats(stats2[:], h2[:]).then_inc(st2_done, 1)

            def post_aggr(c):
                dve.wait_ge(st2_done, c + 1)
                dve.sem_inc(dve_passed, 1)
                v.bn_aggr(mv2[:], stats2[:]).then_inc(mv2_done, 1)

            def post_norm(c):
                dve.wait_ge(rstd2_done, c + 1)
                v.tensor_scalar(x2[:], h2[:], mv2[:, 0:1], rstd2[:, 0:1], ALU.subtract,
                                ALU.mult).then_inc(x2_done, 1)

            def discretize():
                dve.wait_ge(xy_done, NEWTON)
                v.scalar_tensor_tensor(out=AbarT[0:N, :], in0=XY[0:N, 1, :], scalar=2.0, in1=eye[0:N, :],
                                       op0=ALU.mult, op1=ALU.subtract).then_inc(bar_done, 1)
                dve.wait_ge(b_psum, 1)
                v.tensor_scalar(BbarT[:], bank(0)[:, 0:N], dtcol[:, 0:1], None, ALU.mult).then_inc(bar_done, 1)

            for n in range(NG):
                g = n // 2 + 1
                if n == NG - 1:
                    post_norm(0)
                if n:
                    add_rows(n - 1)
                if n % 2 == 1 and g < NP:
                    invert(g, 1)
                if n:
                    moments(n - 1)
                    norm(n - 1)
                if n == SCAN_FROM[0]:
                    discretize()
                if n % 2 == 0 and g < NP:
                    read_spectra(g, 0)
                    add_power(g, 0)
                    read_spectra(g, 1)
                    add_power(g, 1)
                    denominator(g)
                    invert(g, 0)
                if n % 2 == 1 and g < NP:
                    sign(g)
                    if g + 1 < NP:
                        copy_patches(g + 1, 0)
                    angle(g)
                if n == NG - 2:
                    split_weights(dve, v, 1)
                    split_weights(dve, v, 2)
                if n:
                    residual(n - 1)
                if n == NG - 2:
                    post_h2(0, True)
                    post_stats(0)
                    post_aggr(0)
                if n % 2 == 1 and g + 1 < NP:
                    copy_patches(g + 1, 1)

            add_rows(NG - 1)

            def body(c, first, last):
                for j in range(CH):
                    t = CH * c + j
                    h_prev = hseq[:, (j - 1) % CH, :, 1]
                    dve.wait_ge(r_done, t + 1)
                    v.scalar_tensor_tensor(out=rh_hi[:], in0=tanh_r[:], scalar=1.0, in1=h_prev,
                                           op0=ALU.add, op1=ALU.mult).then_inc(rh_hi_done, 1)
                    v.scalar_tensor_tensor(out=rh[:], in0=tanh_r[:], scalar=1.0, in1=h_prev,
                                           op0=ALU.add, op1=ALU.mult).then_inc(rh_full, 1)
                    dve.wait_ge(rh_full, t + 1)
                    v.tensor_tensor(rh_lo[:], rh[:], rh_hi[:], ALU.subtract).then_inc(rh_lo_done, 1)
                    dve.wait_ge(z_done, t + 1)
                    v.tensor_scalar(zgate[:], tanh_z[:], 0.5, 0.5, ALU.mult, ALU.add).then_inc(zg_done, 1)
                    v.tensor_scalar(coef[:, :, 1], tanh_z[:], -0.5 * H_SCALE, 0.5 * H_SCALE, ALU.mult,
                                    ALU.add).then_inc(zh_done, 1)
                    dve.wait_ge(zg_done, t + 1)
                    v.tensor_tensor(addend[:, :, 1], zgate[:], h_prev, ALU.mult).then_inc(zh_done, 1)
                    dve.wait_ge(zh_done, 2 * t + 2)
                    dve.wait_ge(c_done, t + 1)
                    scan(v, h_hi[:].rearrange("p s i -> p (s i)")).then_inc(h_hi_done, 1)
                    if not first and j == 0:
                        dve.wait_ge(hchunk_done, 2 * c - 1)
                    if not first and j == CH // 2:
                        dve.wait_ge(hchunk_done, 2 * c)
                    scan(v, hseq[:, j].rearrange("p s i -> p (s i)")).then_inc(h_full, 1)
                    dve.wait_ge(h_full, t + 1)
                    v.tensor_tensor(h_lo[:], hseq[:, j, :, 1], h_hi[:, :, 1],
                                    ALU.subtract).then_inc(h_lo_done, 1)
                    if first and j == 0:
                        moments(NG - 1)
                    if first and j == LAST_ROWS_AT - 1:
                        norm(NG - 1)
                    if first and j == LAST_ROWS_AT + 3:
                        residual(NG - 1)
                    if not last and j == 0:
                        post_h2(c + 1, False)
                    if not last and j == 1:
                        post_stats(c + 1)
                    if not last and j == 2:
                        post_aggr(c + 1)
                    if not last and j == NORM_AT:
                        post_norm(c + 1)
                    if not first and j == LOGIT_AT:
                        dve.wait_ge(o_psum, c)
                        v.tensor_tensor(logit[:], ps_o, bo_bc[:], ALU.add).then_inc(logit_done, 1)

            body(0, True, False)
            with dve.Fori(1, NCH - 1) as c:
                body(c, False, False)
            body(NCH - 1, False, True)
            dve.wait_ge(o_psum, NCH)
            v.tensor_tensor(logit[:], ps_o, bo_bc[:], ALU.add).then_inc(logit_done, 1)

        @block.tensor
        def _(pe):
            mm, tr = nc.tensor.matmul, nc.tensor.transpose

            def transposes(g, h):
                s0, s1, cols = patches(h)
                if h == 0:
                    pe.wait_ge(x_in[g], 16)
                if 2 * g + h > 1:
                    pe.wait_ge(patT0_copied, 2 * g + h)
                    pe.wait_ge(patT1_copied, 2 * g + h)
                for k in range(2):
                    for sg in range(s0, s1):
                        n0 = sg * PATCH + k * KP
                        last = tr(ps_patT(k, g, h)[:, (sg - s0) * 128:(sg - s0 + 1) * 128],
                                  x_sb[:, g, n0:n0 + KP], ident[:])
                last.then_inc(patT_psum, 1)

            def spectra(g, h):
                if h == 0:
                    if g == 0:
                        pe.wait_ge(dft_in, 16)
                    pe.wait_ge(patT0_copied, 2 * g + 2)
                    pe.wait_ge(patT1_copied, 2 * g + 2)
                if 2 * g + h > 1:
                    pe.wait_ge(re_read, 2 * g + h)
                    pe.wait_ge(im_read, 2 * g + h)
                for part, dst in ((0, ps_re(g, h)), (1, ps_im(g, h))):
                    for k in range(2):
                        v = patT[:, k, :].rearrange("p (s b c) -> p c s b", s=NS, b=NB)
                        last = mm(dst, dft_sb[:, k, part, :], v[:, h * (CP // 2):(h + 1) * (CP // 2)],
                                  start=k == 0, stop=k == 1)
                last.then_inc(spec_psum, 1)

            def wait_newton(i):
                pe.wait_ge(xy_done if i % 2 else dn_done, i // 2 + 1)

            def newton(i):
                ps_nt, ps_nx = newton_bank(i)
                if i:
                    wait_newton(i - 1)
                if i % 2 == 0:
                    mm(ps_nt, eye2[:], eye[:], start=True, stop=False)
                    mm(ps_nt, negMT[:], XY[:, 0, :], start=False, stop=True).then_inc(nt_psum, 1)
                else:
                    mm(ps_nx[:, 0:N], XY[:, 1, :], Dn[:], start=True, stop=True)
                    mm(ps_nx[:, N:2 * N], Dn[:], XY[:, 1, :], start=True, stop=True).then_inc(nx_psum, 1)

            pe.wait_ge(consts, 1)
            for _ in range(WARM):
                tr(bank(6)[:, 0:128], ident[:], ident[:])
            for h in range(2):
                transposes(0, h)
            spectra(0, 0)
            pe.wait_ge(su_dve, 2)
            pe.wait_ge(consts, 14)
            mm(bank(5)[:, 0:1], ones_row[:], dtsum[:], start=True, stop=True).then_inc(su_pe, 1)
            spectra(0, 1)
            pe.wait_ge(su_dve, 9)
            mm(bank(5)[0:N, 0:1], ones_sq[:], sqsum[:], start=True, stop=True).then_inc(sq_psum, 1)
            transposes(1, 0)
            pe.wait_ge(ssm_in, 16 * 7)
            pe.wait_ge(re_read, 1)
            mm(bank(2)[:, 0:3 * DM], ones_row[:], vec_rows[:].rearrange("p a d -> p (a d)"),
               start=True, stop=True).then_inc(su_pe, 1)
            pe.wait_ge(su_dve, 11)
            tr(bank(5)[:, 0:128], Wout_sb[:], ident[:]).then_inc(su_pe, 1)
            pe.wait_ge(im_read, 2)
            for i in range(EARLY):
                newton(i)
            pe.wait_ge(rows_in, 16 * 8)
            tr(bank(4)[:, 0:32], bias_rows[:], ident[0:32, 0:32]).then_inc(bias_psum, 1)
            transposes(1, 1)
            pe.wait_ge(su_act, 6)

            def ssm_input(c, half):
                mm(ps_s[half], BbarT[:], xlnT[:, bass.ds(c * CT + half * (CT // 2), CT // 2)], start=True,
                   stop=False, skip_group_check=True)

            def ssm_step(c, k, first=False):
                if not first:
                    pe.wait_ge(s_done, CH * c + k)
                k0, k1 = (k - 1) % CH, k % (CH // 2)
                mm(ps_s[k // (CH // 2)][:, k1 * NB:(k1 + 1) * NB], AbarT[:], states[:, k0 * NB:(k0 + 1) * NB],
                   start=False, stop=(k1 == CH // 2 - 1), skip_group_check=True).then_inc(s_psum, 1)

            def ssm_out(c, first):
                pe.wait_ge(s_done, CH * (c + 1))
                if not first:
                    pe.wait_ge(gin_done, 3 * KH * c)
                mm(ps_p, states[0:N, :], WCT[:], start=True, stop=True).then_inc(p_psum, 1)

            def transpose_x2(c):
                pe.wait_ge(x2_done, c + 1)
                tr(ps_p, x2[:], ident[:]).then_inc(x2T_psum, 1)

            def gate_inputs(c, i, first):
                if i == 0:
                    pe.wait_ge(x2T_done, c + 1)
                    if not first:
                        pe.wait_ge(gin_done, 3 * KH * c)
                if i >= 2:
                    pe.wait_ge(gin_done, 3 * KH * c + i - 1)
                mm(ps_x[i % 2], WuT[:, i, :], x2T[:], start=True, stop=True).then_inc(gx_psum, 1)

            def transpose_weights(i):
                b = WEIGHT_BANKS[i]
                if i == 0:
                    pe.wait_ge(gru_in, 16 * 7)
                    pe.wait_ge(su_dve, 15)
                    pe.wait_ge(re_read, 2 * NP)
                    pe.wait_ge(im_read, 2 * NP)
                if i >= 2:
                    pe.wait_ge(wT_done, i - 1)
                if i < 3:
                    for k in range(KH):
                        for m in range(KH):
                            last = tr(bank(b)[:, k * H + m * 128:k * H + (m + 1) * 128],
                                      wnat[:, i, m, k * 128:(k + 1) * 128], ident[:])
                elif i == 3:
                    for u in range(4):
                        last = tr(bank(b)[:, u * 128:(u + 1) * 128], wunat[:, u // 2, u % 2, :], ident[:])
                else:
                    for u in range(4, 6):
                        tr(bank(b)[:, (u - 4) * 128:(u - 3) * 128], wunat[:, u // 2, u % 2, :], ident[:])
                    for k in range(KH):
                        last = tr(bank(b)[:, 256 + k * 128:384 + k * 128], wonat[:, k * 128:(k + 1) * 128],
                                  ident[:])
                last.then_inc(su_pe, 1)

            def serial(n, m, slot):
                if (n, m, slot) in SLOTS:
                    i = SLOTS[n, m, slot]
                    if n % 2 and (m, slot) == (0, 0):
                        pe.wait_ge(re_read, min(n + 3, 2 * NP))
                    if n and n % 2 == 0 and (m, slot) == (0, 0):
                        pe.wait_ge(y0_read, n - 1)
                    newton(i)
                if (n, m, slot) in SCANS:
                    k = SCANS[n, m, slot]
                    if k == 0:
                        pe.wait_ge(bar_done, 2)
                        pe.wait_ge(wct_done, 1)
                        ssm_input(0, 0)
                        ssm_input(0, 1)
                    if k == CH:
                        pe.wait_ge(wT_done, 5)
                        ssm_out(0, True)
                        ssm_input(1, 0)
                        ssm_input(1, 1)
                    ssm_step(k // CH, k % CH, k == 0)

            def up(n, m, half):
                t0, nq = group(n)
                p = MC * n + m
                k = msize(m)
                feats = (magT, angT)[half]
                last = mm(ps_hid[p % 2][0:k, 0:nq * CT], W1_sb[:, half, m * 128:m * 128 + k],
                          feats[:, t0:t0 + nq * CT], start=half == 0, stop=half == 1)
                if half == 1:
                    last.then_inc(hid_psum, 1)

            def down(n, m):
                nq = group(n)[1]
                p = MC * n + m
                k = msize(m)
                if m == 0 and n:
                    pe.wait_ge(out_read, n)
                pe.wait_ge(gelu_done, p + 1)
                for q in range(nq):
                    last = mm(ps_out[:, q * DM:(q + 1) * DM], hid[0:k, p % 2, q * 128:(q + 1) * 128],
                              W2_sb[0:k, m, :], start=(m == 0 and q == 0), stop=(m == MC - 1),
                              skip_group_check=True)
                if m == MC - 1:
                    last.then_inc(out_psum, 1)

            def transpose_x(n):
                pe.wait_ge(xln_done, n + 1)
                if n:
                    pe.wait_ge(y0_read, n)
                for q in range(group(n)[1]):
                    last = tr(ps_row[:, q * 128:(q + 1) * 128], xln[:, q, :], ident[:])
                last.then_inc(xT_psum, 1)

            def skip(n):
                t0, nq = group(n)
                pe.wait_ge(xT_copied, n + 1)
                for q in range(nq):
                    last = mm(ps_row[:, q * DM:(q + 1) * DM], xlnT[:, t0 + q * CT:t0 + (q + 1) * CT], WDT[:],
                              start=(q == 0), stop=(q == nq - 1), skip_group_check=True)
                last.then_inc(y0_psum, 1)

            pe.wait_ge(su_dve, 13)
            for n in range(NG):
                g = n // 2 + 1
                shared = n % 2 == 0 and n < NG - 2 and n > 0
                if n % 2 == 0:
                    pe.wait_ge(ang_done, n // 2 + 1)
                for m in range(MC):
                    up(n, m, 0)
                    if shared and m == XT_PIECE + 1:
                        pe.wait_ge(xT_copied, n)
                    serial(n, m, 0)
                    up(n, m, 1)
                    if n % 2 == 0 and g < NP and m in (0, 2):
                        if m == 0 and n:
                            wait_newton(SLOTS[n, 0, 0] - 1)
                        spectra(g, m // 2)
                    if n and m == XT_PIECE:
                        if shared:
                            wait_newton(SLOTS[n, m, 0])
                        transpose_x(n - 1)
                    if n and m == SKIP_PIECE:
                        if shared:
                            wait_newton(SLOTS[n, m - 1, 2])
                        skip(n - 1)
                    if n == NG - 1 and m == 0:
                        transpose_x2(0)
                    if n == NG - 1 and m in FIRST_GATES:
                        for i in FIRST_GATES[m]:
                            gate_inputs(0, i, True)
                    if n % 2 == 1 and g + 1 < NP and m in (3, 5):
                        transposes(g + 1, (m - 3) // 2)
                    if (n, m + 1) in WEIGHTS_AT or (m == MC - 1 and (n + 1, 0) in WEIGHTS_AT):
                        transpose_weights(WEIGHTS_AT[(n, m + 1) if m < MC - 1 else (n + 1, 0)])
                    serial(n, m, 1)
                    if m:
                        down(n, m - 1)
                    elif n:
                        down(n - 1, MC - 1)
                    serial(n, m, 2)
                    if (n, m + 1) == SCAN_FROM:
                        pe.wait_ge(xy_done, NEWTON)
                        mm(bank(0)[:, 0:N], B_sb[:], XY[0:N, 1, :], start=True, stop=True).then_inc(b_psum, 1)
                        mm(bank(3)[0:N, 0:DM], C_sb[:], WoutT[:], start=True, stop=True).then_inc(c_w_psum, 1)
            down(NG - 1, MC - 1)

            def place_inputs(c, j, g):
                if j % (CH // 2) == 0:
                    pe.wait_ge(gp_chain, 24 * c + 12 * (j // (CH // 2)) + 4 * g + 4)
                for i in range(3):
                    mm(ps_gate[g], ident_bf[:], gparts[:, i, j, g, :], start=(i == 0), stop=False,
                       skip_group_check=True)

            def recur_hi(g, state):
                for m in range(KH):
                    for k in range(KH):
                        for w in (w_first[:, g, k], w_rest[:, 0, g, k], w_rest[:, 1, g, k]):
                            mm(ps_gate[g][:, gate_cols(m)], w[:, m * 128:(m + 1) * 128],
                               state[:, k * NB:(k + 1) * NB], start=False, stop=False, skip_group_check=True)

            def recur_lo(g, state):
                for m in range(KH):
                    for k in range(KH):
                        last = mm(ps_gate[g][:, gate_cols(m)], w_first[:, g, k, m * 128:(m + 1) * 128],
                                  state[:, k * NB:(k + 1) * NB], start=False, stop=(m, k) == (KH - 1, KH - 1),
                                  skip_group_check=True)
                return last

            def output_product(c, k):
                if k == 0:
                    pe.wait_ge(hchunk_done, 2 * c + 2)
                last = mm(ps_o, hchunk[:, k].rearrange("p t b -> p (t b)"), WoT[:, k, :],
                          start=k == 0, stop=k == KH - 1)
                if k == KH - 1:
                    last.then_inc(o_psum, 1)

            ssm_out(1, False)
            ssm_input(2, 0)
            ssm_input(2, 1)
            ssm_step(2, 0)
            for g in range(3):
                pe.wait_ge(wp_done[g], 4)
            place_inputs(0, 0, 0)
            place_inputs(0, 0, 1)

            def body(c, out_before, post_next, scan_2, scan_3):
                for j in range(CH):
                    t = CH * c + j
                    start_of_all = not out_before and j == 0
                    if not start_of_all:
                        pe.wait_ge(h_hi_done, t)
                    recur_hi(0, h_hi[:, :, 1])
                    if not start_of_all:
                        pe.wait_ge(h_lo_done, t)
                    recur_lo(0, h_lo[:]).then_inc(r_psum, 1)
                    if start_of_all:
                        pe.wait_ge(out_read, NG)
                    else:
                        pe.wait_ge(c_done, t)
                    place_inputs(c, j, 2)
                    recur_hi(1, h_hi[:, :, 1])
                    recur_lo(1, h_lo[:]).then_inc(z_psum, 1)
                    if scan_2 and j < CH - 1:
                        ssm_step(c + 2, j + 1)
                    if scan_3 and j == CH - 1:
                        ssm_step(c + 3, 0)
                    pe.wait_ge(rh_hi_done, t + 1)
                    recur_hi(2, rh_hi[:])
                    pe.wait_ge(rh_lo_done, t + 1)
                    recur_lo(2, rh_lo[:]).then_inc(c_psum, 1)
                    if post_next or j < CH - 1:
                        pe.wait_ge(r_done, t + 1)
                        pe.wait_ge(z_done, t + 1)
                        nxt = (c, j + 1) if j < CH - 1 else (c + 1, 0)
                        place_inputs(*nxt, 0)
                        place_inputs(*nxt, 1)
                    if scan_2 and out_before and j == 1:
                        ssm_input(c + 2, 1)
                    if not out_before and j == LAST_ROWS_AT:
                        transpose_x(NG - 1)
                    if not out_before and j == LAST_ROWS_AT + 2:
                        skip(NG - 1)
                    if out_before and j in (OUT_AT, OUT_AT + 1):
                        output_product(c - 1, j - OUT_AT)
                    if post_next and j == TRANSPOSE_AT:
                        transpose_x2(c + 1)
                    if post_next and 0 <= j - GATES_AT < 3 * KH:
                        gate_inputs(c + 1, j - GATES_AT, False)
                    if scan_3 and j == CH - 3:
                        ssm_input(c + 3, 0)
                    if scan_2 and j == CH - 2:
                        ssm_out(c + 2, False)

            body(0, False, True, True, True)
            with pe.Fori(1, NCH - 3) as c:
                body(c, True, True, True, True)
            body(NCH - 3, True, True, True, False)
            body(NCH - 2, True, True, False, False)
            body(NCH - 1, True, False, False, False)
            output_product(NCH - 1, 0)
            output_product(NCH - 1, 1)


_INS = ["x", "L0_tok_W1", "L0_tok_b1", "L0_tok_W2", "L0_tok_b2", "L0_attn_A", "L0_attn_B", "L0_attn_C",
        "L0_attn_D", "L0_attn_log_dt", "L0_attn_W_out", "L0_attn_b_out", "L0_ffn_Wuz", "L0_ffn_buz",
        "L0_ffn_Wwz", "L0_ffn_bwz", "L0_ffn_Wur", "L0_ffn_bur", "L0_ffn_Wwr", "L0_ffn_bwr", "L0_ffn_Wu",
        "L0_ffn_bu", "L0_ffn_Ww", "L0_ffn_bw", "L0_ffn_Wo", "L0_ffn_bo"]
_PATCH = 200


def _dft_table():
    import numpy as np
    n = np.arange(_PATCH)[:, None]
    f = np.arange(_PATCH // 2 + 1)[None, :]
    k = (n * f) % _PATCH
    cos = np.cos(2 * np.pi * k / _PATCH)
    sin = -np.sin(2 * np.pi * k / _PATCH)
    sin[(2 * k) % _PATCH == 0] = 0.0
    both = np.stack([cos, sin], axis=1).reshape(2, _PATCH // 2, 2, _PATCH // 2 + 1)
    return np.ascontiguousarray(both.transpose(1, 0, 2, 3).astype(np.float32))


def kernel(**inputs):
    import numpy as _np
    import concourse.bacc as _bacc
    from concourse import mybir as _mybir
    from concourse.bass_utils import run_bass_kernel_spmd as _run

    nc = _bacc.Bacc("TRN2", target_bir_lowering=False, num_devices=1)
    arrays, args = {}, []
    for name in _INS:
        arrays[f"in_{name}"] = _np.ascontiguousarray(inputs[name])
    arrays["in_dft"] = _dft_table()
    for name, a in arrays.items():
        args.append(nc.dram_tensor(name, a.shape, _mybir.dt.from_np(a.dtype), kind="ExternalInput").ap())
    b, c, n = inputs["x"].shape
    shape = (b, c * (n // _PATCH), inputs["L0_tok_W2"].shape[1])
    args.append(nc.dram_tensor("out_0", shape, _mybir.dt.float32, kind="ExternalOutput").ap())
    audio_tower(nc, *args)
    r = _run(nc, [arrays], core_ids=[0])
    return r.results[0]["out_0"]
```
